# Optimizing a Trainium2 kernel written in Bass

```python
import numpy as np
import jax
import jax.numpy as jnp

def _softmax(x, axis=-1):
    return jax.nn.softmax(x, axis=axis)
def _gelu(x):
    return jax.nn.gelu(x, approximate=True)
def _silu(x):
    return jax.nn.silu(x)
def _sigmoid(x):
    return jax.nn.sigmoid(x)
def _layernorm(x, axis=-1, eps=1e-5):
    m = jnp.mean(x, axis=axis, keepdims=True)
    v = jnp.var(x, axis=axis, keepdims=True)
    return (x - m) / jnp.sqrt(v + eps)
def _scatter_add(tgt, idx, src, axis=0):
    return tgt.at[idx].add(src)
def _segment_sum(src, seg, n):
    return jax.ops.segment_sum(src, seg, n)

kernel_name = 'mk_metaformer_d2_conv_nhwc128_5f3189'

def setup_inputs(seed: int = 0):
    np.random.seed(seed)
    _w = jnp.asarray
    def _rec_inputs():
        import jax
        import jax.numpy as jnp
        _gk = jax.random.key(seed)
        x = -0.0002091 + 1 * jax.random.normal(jax.random.fold_in(_gk, 1), (64, 56, 56, 128), jnp.float32)
        return x
    x = _rec_inputs()
    def _L0_conv_setup():
        import jax, jax.numpy as jnp
        import numpy as np
        WINDOW = 7
        SHIFT = 3
        HEADS = 4

        def _rel_pos_index(w):
            coords = np.stack(np.meshgrid(np.arange(w), np.arange(w), indexing='ij'))
            cf = coords.reshape(2, -1)
            rc = (cf[:, :, None] - cf[:, None, :]).transpose(1, 2, 0)
            rc[:, :, 0] += w - 1
            rc[:, :, 1] += w - 1
            rc[:, :, 0] *= 2 * w - 1
            return rc.sum(-1).reshape(-1)

        def _attn_mask(H, W, w, s):
            m = np.zeros((H, W))
            slices = ((0, -w), (-w, -s), (-s, None))
            cnt = 0
            for hs in slices:
                for ws in slices:
                    m[hs[0]:hs[1], ws[0]:ws[1]] = cnt
                    cnt += 1
            m = m.reshape(H // w, w, W // w, w).transpose(0, 2, 1, 3).reshape(-1, w * w)
            d = m[:, None, :] - m[:, :, None]
            return np.where(d != 0, -100.0, 0.0).astype(np.float32)
        key = jax.random.key(seed)
        ks = jax.random.split(key, 6)
        B, H, W, C = (64, 56, 56, 128)
        return {'x': jax.random.normal(ks[0], (B, H, W, C), dtype=jnp.float32), 'qkv_weight': jax.random.normal(ks[1], (3 * C, C), dtype=jnp.float32) * 0.02, 'qkv_bias': jax.random.normal(ks[2], (3 * C,), dtype=jnp.float32) * 0.02, 'proj_weight': jax.random.normal(ks[3], (C, C), dtype=jnp.float32) * 0.02, 'proj_bias': jax.random.normal(ks[4], (C,), dtype=jnp.float32) * 0.02, 'rel_bias_table': jax.random.normal(ks[5], ((2 * WINDOW - 1) ** 2, HEADS), dtype=jnp.float32) * 0.02}
    _L0_conv_all = _L0_conv_setup()
    _L0_conv_in = {k: v for k, v in _L0_conv_all.items() if k in ('qkv_weight', 'qkv_bias', 'proj_weight', 'proj_bias', 'rel_bias_table', )}
    del _L0_conv_all

    def _L0_ffn_setup():
        import jax, jax.numpy as jnp
        import numpy as np
        BN_EPS = 1e-05
        key = jax.random.key(seed)
        k1, k2, k3 = jax.random.split(key, 3)
        B, T, I, H = (64, 2048, 128, 128)
        x = jax.random.normal(k1, (B, T, I), dtype=jnp.float32)
        W = jax.random.normal(k2, (H, I), dtype=jnp.float32) * (1.0 / np.sqrt(I))
        V = jnp.linalg.qr(jax.random.normal(k3, (H, H), dtype=jnp.float32))[0]
        gamma = jnp.ones((H,), dtype=jnp.float32)
        beta = jnp.zeros((H,), dtype=jnp.float32)
        return {'x': x, 'W': W, 'V': V, 'gamma': gamma, 'beta': beta}
    _L0_ffn_all = _L0_ffn_setup()
    _L0_ffn_in = {k: v for k, v in _L0_ffn_all.items() if k in ('W', 'V', 'gamma', 'beta', )}
    del _L0_ffn_all

    def _L1_conv_setup():
        import jax, jax.numpy as jnp
        import numpy as np
        B, H, W, C, K, T = (16, 128, 128, 64, 7, 16)
        C2 = 2 * C

        def _pad_and_fft(kr, ki, h, w, k):
            kern = kr + 1j * ki
            ph = (h - k) // 2
            pw = (w - k) // 2
            padded = jnp.pad(kern, ((0, 0), (ph, h - k - ph), (pw, w - k - pw)))
            return jnp.fft.fft2(padded, axes=(-2, -1))
        key = jax.random.key(seed)
        ks = jax.random.split(key, 12)
        d = {'x_ri': jax.random.normal(ks[0], (B, H, W, C2), jnp.float32), 'Wf': jax.random.normal(ks[1], (C2, C2), jnp.float32) * 0.05, 'bf': jnp.zeros((C2,), jnp.float32), 'Wi': jax.random.normal(ks[2], (C2, C2), jnp.float32) * 0.05, 'bi': jnp.zeros((C2,), jnp.float32), 'Wd': jax.random.normal(ks[3], (C2, C2), jnp.float32) * 0.05, 'bd': jnp.zeros((C2,), jnp.float32), 'A_real': jax.random.normal(ks[4], (C, K, K), jnp.float32) * 0.02, 'A_imag': jax.random.normal(ks[5], (C, K, K), jnp.float32) * 0.02, 'B_real': jax.random.normal(ks[6], (C, K, K), jnp.float32) * 0.02, 'B_imag': jax.random.normal(ks[7], (C, K, K), jnp.float32) * 0.02}
        return d
    _L1_conv_all = _L1_conv_setup()
    _L1_conv_in = {k: v for k, v in _L1_conv_all.items() if k in ('Wf', 'bf', 'Wi', 'bi', 'Wd', 'bd', 'A_real', 'A_imag', 'B_real', 'B_imag', )}
    del _L1_conv_all

    def _L1_ffn_setup():
        import jax, jax.numpy as jnp
        import numpy as np
        B, S, D, E, H, O, K = (512, 2048, 128, 64, 512, 128, 8)
        key = jax.random.key(seed)
        k0, k1, k2, k3 = jax.random.split(key, 4)
        x = jax.random.normal(k0, (B, S, D), dtype=jnp.float32)
        gate_w = jax.random.normal(k1, (E, D), dtype=jnp.float32) * (1.0 / np.sqrt(D))
        gate_b = jnp.zeros((E,), dtype=jnp.float32)
        weight1 = jax.random.uniform(k2, (E, D + 1, H), dtype=jnp.float32, minval=-1.0, maxval=1.0) * (1.0 / np.sqrt(D + 1))
        weight2 = jax.random.uniform(k3, (E, H + 1, O), dtype=jnp.float32, minval=-1.0, maxval=1.0) * (1.0 / np.sqrt(H + 1))
        return {'x': x, 'gate_w': gate_w, 'gate_b': gate_b, 'weight1': weight1, 'weight2': weight2}
    _L1_ffn_all = _L1_ffn_setup()
    _L1_ffn_in = {k: v for k, v in _L1_ffn_all.items() if k in ('gate_w', 'gate_b', 'weight1', 'weight2', )}
    del _L1_ffn_all

    return {
        "x": x,
        "L0_conv_qkv_weight": _L0_conv_in["qkv_weight"],
        "L0_conv_qkv_bias": _L0_conv_in["qkv_bias"],
        "L0_conv_proj_weight": _L0_conv_in["proj_weight"],
        "L0_conv_proj_bias": _L0_conv_in["proj_bias"],
        "L0_conv_rel_bias_table": _L0_conv_in["rel_bias_table"],
        "L0_ffn_W": _L0_ffn_in["W"],
        "L0_ffn_V": _L0_ffn_in["V"],
        "L0_ffn_gamma": _L0_ffn_in["gamma"],
        "L0_ffn_beta": _L0_ffn_in["beta"],
        "L1_conv_Wf": _L1_conv_in["Wf"],
        "L1_conv_bf": _L1_conv_in["bf"],
        "L1_conv_Wi": _L1_conv_in["Wi"],
        "L1_conv_bi": _L1_conv_in["bi"],
        "L1_conv_Wd": _L1_conv_in["Wd"],
        "L1_conv_bd": _L1_conv_in["bd"],
        "L1_conv_A_real": _L1_conv_in["A_real"],
        "L1_conv_A_imag": _L1_conv_in["A_imag"],
        "L1_conv_B_real": _L1_conv_in["B_real"],
        "L1_conv_B_imag": _L1_conv_in["B_imag"],
        "L1_ffn_gate_w": _L1_ffn_in["gate_w"],
        "L1_ffn_gate_b": _L1_ffn_in["gate_b"],
        "L1_ffn_weight1": _L1_ffn_in["weight1"],
        "L1_ffn_weight2": _L1_ffn_in["weight2"],
    }

def reference(x, L0_conv_qkv_weight, L0_conv_qkv_bias, L0_conv_proj_weight, L0_conv_proj_bias, L0_conv_rel_bias_table, L0_ffn_W, L0_ffn_V, L0_ffn_gamma, L0_ffn_beta, L1_conv_Wf, L1_conv_bf, L1_conv_Wi, L1_conv_bi, L1_conv_Wd, L1_conv_bd, L1_conv_A_real, L1_conv_A_imag, L1_conv_B_real, L1_conv_B_imag, L1_ffn_gate_w, L1_ffn_gate_b, L1_ffn_weight1, L1_ffn_weight2):
    import jax
    import jax.numpy as jnp
    def _L0_conv_ref(x, qkv_weight, qkv_bias, proj_weight, proj_bias, rel_bias_table):
        import jax, jax.numpy as jnp
        import numpy as np
        WINDOW = 7
        SHIFT = 3
        HEADS = 4

        def _rel_pos_index(w):
            coords = np.stack(np.meshgrid(np.arange(w), np.arange(w), indexing='ij'))
            cf = coords.reshape(2, -1)
            rc = (cf[:, :, None] - cf[:, None, :]).transpose(1, 2, 0)
            rc[:, :, 0] += w - 1
            rc[:, :, 1] += w - 1
            rc[:, :, 0] *= 2 * w - 1
            return rc.sum(-1).reshape(-1)

        def _attn_mask(H, W, w, s):
            m = np.zeros((H, W))
            slices = ((0, -w), (-w, -s), (-s, None))
            cnt = 0
            for hs in slices:
                for ws in slices:
                    m[hs[0]:hs[1], ws[0]:ws[1]] = cnt
                    cnt += 1
            m = m.reshape(H // w, w, W // w, w).transpose(0, 2, 1, 3).reshape(-1, w * w)
            d = m[:, None, :] - m[:, :, None]
            return np.where(d != 0, -100.0, 0.0).astype(np.float32)
        B, H, W, C = x.shape
        w, s, h = (WINDOW, SHIFT, HEADS)
        d = C // h
        nH, nW = (H // w, W // w)
        nwin = nH * nW
        L = w * w
        bias = rel_bias_table[jnp.asarray(_rel_pos_index(w))].reshape(L, L, h).transpose(2, 0, 1)
        xs = jnp.roll(x, (-s, -s), axis=(1, 2))
        xw = xs.reshape(B, nH, w, nW, w, C).transpose(0, 1, 3, 2, 4, 5).reshape(B * nwin, L, C)
        qkv = (xw @ qkv_weight.T + qkv_bias).reshape(B * nwin, L, 3, h, d).transpose(2, 0, 3, 1, 4)
        q, k, v = (qkv[0] * d ** (-0.5), qkv[1], qkv[2])
        attn = jnp.einsum('nhqd,nhkd->nhqk', q, k) + bias[None]
        mask = jnp.asarray(_attn_mask(H, W, w, s))
        attn = attn.reshape(B, nwin, h, L, L) + mask[None, :, None]
        attn = jax.nn.softmax(attn.reshape(B * nwin, h, L, L), axis=-1)
        out = jnp.einsum('nhqk,nhkd->nhqd', attn, v).transpose(0, 2, 1, 3).reshape(B * nwin, L, C)
        out = out @ proj_weight.T + proj_bias
        out = out.reshape(B, nH, nW, w, w, C).transpose(0, 1, 3, 2, 4, 5).reshape(B, H, W, C)
        return jnp.roll(out, (s, s), axis=(1, 2))

    def _L0_ffn_ref(x, W, V, gamma, beta):
        import jax, jax.numpy as jnp
        import numpy as np
        BN_EPS = 1e-05
        B, T, H = (x.shape[0], x.shape[1], W.shape[0])
        Wx = jnp.einsum('bti,hi->bth', x, W)
        flat = Wx.reshape(B * T, H)
        mean = jnp.mean(flat, axis=0)
        var = jnp.var(flat, axis=0)
        Wx = ((flat - mean) * jax.lax.rsqrt(var + BN_EPS) * gamma + beta).reshape(B, T, H)
        Vt = V.T

        def step(yt, wx_t):
            yt = jax.nn.sigmoid(wx_t + yt @ Vt)
            return (yt, yt)
        y0 = jnp.zeros((B, H), dtype=Wx.dtype)
        _, ys = jax.lax.scan(step, y0, jnp.swapaxes(Wx, 0, 1))
        return jnp.swapaxes(ys, 0, 1)

    def _L1_conv_ref(x_ri, Wf, bf, Wi, bi, Wd, bd, A_real, A_imag, B_real, B_imag):
        import jax, jax.numpy as jnp
        import numpy as np
        B, H, W, C, K, T = (16, 128, 128, 64, 7, 16)
        C2 = 2 * C

        def _pad_and_fft(kr, ki, h, w, k):
            kern = kr + 1j * ki
            ph = (h - k) // 2
            pw = (w - k) // 2
            padded = jnp.pad(kern, ((0, 0), (ph, h - k - ph), (pw, w - k - pw)))
            return jnp.fft.fft2(padded, axes=(-2, -1))
        b, h, w, c2 = x_ri.shape
        c = c2 // 2
        k = A_real.shape[-1]
        forget_gate = jax.nn.sigmoid(x_ri @ Wf + bf + 2.0)
        input_gate = jax.nn.sigmoid(x_ri @ Wi + bi)
        delta = jax.nn.softplus(x_ri @ Wd + bd) * 0.1
        A_f = _pad_and_fft(A_real, A_imag, h, w, k)
        B_f = _pad_and_fft(B_real, B_imag, h, w, k)
        A_ri = jnp.concatenate([A_f.real, A_f.imag], 0).transpose(1, 2, 0)[None]
        B_ri = jnp.concatenate([B_f.real, B_f.imag], 0).transpose(1, 2, 0)[None]
        Ar, Ai = (A_ri[..., :c], A_ri[..., c:])
        mag = jnp.sqrt(Ar ** 2 + Ai ** 2 + 1e-08)
        scale = 0.95 * jax.nn.sigmoid(mag) / (mag + 1e-08)
        Ar = Ar * scale
        Ai = Ai * scale
        Br, Bi_ = (B_ri[..., :c], B_ri[..., c:])
        x_r, x_i = (x_ri[..., :c], x_ri[..., c:])
        Bx_r = Br * x_r - Bi_ * x_i
        Bx_i = Br * x_i + Bi_ * x_r
        inp_r = delta[..., :c] * input_gate[..., :c] * Bx_r
        inp_i = delta[..., c:] * input_gate[..., c:] * Bx_i
        fg_r, fg_i = (forget_gate[..., :c], forget_gate[..., c:])

        def step(h_state, _):
            h_r, h_i = h_state
            Ah_r = Ar * h_r - Ai * h_i
            Ah_i = Ar * h_i + Ai * h_r
            return ((fg_r * Ah_r + inp_r, fg_i * Ah_i + inp_i), None)
        h0 = (jnp.zeros_like(x_r), jnp.zeros_like(x_i))
        (h_r, h_i), _ = jax.lax.scan(step, h0, None, length=T)
        return jnp.concatenate([h_r, h_i], axis=-1)

    def _L1_ffn_ref(x, gate_w, gate_b, weight1, weight2):
        import jax, jax.numpy as jnp
        import numpy as np
        B, S, D, E, H, O, K = (512, 2048, 128, 64, 512, 128, 8)
        Bn, Sn, Dn = x.shape
        logits = jnp.einsum('bsd,ed->bse', x, gate_w) + gate_b
        probs = jax.nn.softmax(logits, axis=1)
        vals, idx = jax.lax.top_k(probs.transpose(0, 2, 1), K)
        topv = vals.transpose(0, 2, 1)
        topi = idx.transpose(0, 2, 1)
        flat_idx = topi.reshape(Bn, K * E)
        gathered = jnp.take_along_axis(x, flat_idx[:, :, None], axis=1)
        gathered = gathered.reshape(Bn, K, E, Dn)
        pooled = jnp.einsum('bked,bke->bed', gathered, topv)
        ones = jnp.ones((E, Bn, 1), dtype=x.dtype)
        h = jnp.concatenate([pooled.transpose(1, 0, 2), ones], axis=-1)
        h = jax.nn.gelu(jnp.einsum('ebd,edh->ebh', h, weight1), approximate=False)
        h = jnp.concatenate([h, ones], axis=-1)
        out = jnp.einsum('ebh,eho->ebo', h, weight2)
        out = out.transpose(1, 0, 2)
        weighted = jnp.einsum('beo,bke->bkeo', out, topv).reshape(Bn, K * E, O)
        outputs = jnp.zeros((Bn, Sn, O), dtype=x.dtype)
        outputs = outputs.at[jnp.arange(Bn)[:, None], flat_idx].add(weighted)
        return outputs

    def _gn(v, G=32, eps=1e-5):
        B_, H_, W_, C_ = v.shape
        g = v.reshape(B_, H_, W_, G, C_ // G)
        m = jnp.mean(g, axis=(1, 2, 4), keepdims=True)
        s = jnp.var(g, axis=(1, 2, 4), keepdims=True)
        return ((g - m) / jnp.sqrt(s + eps)).reshape(v.shape)

    def _ln_c(v, eps=1e-6):
        m = jnp.mean(v, axis=-1, keepdims=True)
        s = jnp.var(v, axis=-1, keepdims=True)
        return (v - m) / jnp.sqrt(s + eps)

    def _ln_t(v, eps=1e-5):
        m = jnp.mean(v, axis=-1, keepdims=True)
        s = jnp.var(v, axis=-1, keepdims=True)
        return (v - m) / jnp.sqrt(s + eps)

    def _to_tokens(v):
        B_, H_, W_, C_ = v.shape
        return v.reshape(B_, H_ * W_, C_)
    def _from_tokens(t, like):
        return t.reshape(like.shape)

    x = x + _L0_conv_ref(_ln_c(x), L0_conv_qkv_weight, L0_conv_qkv_bias, L0_conv_proj_weight, L0_conv_proj_bias, L0_conv_rel_bias_table)
    t = _to_tokens(x)
    t = t + _L0_ffn_ref(_ln_t(t), L0_ffn_W, L0_ffn_V, L0_ffn_gamma, L0_ffn_beta)
    x = _from_tokens(t, x)
    x = x + _L1_conv_ref(_ln_c(x), L1_conv_Wf, L1_conv_bf, L1_conv_Wi, L1_conv_bi, L1_conv_Wd, L1_conv_bd, L1_conv_A_real, L1_conv_A_imag, L1_conv_B_real, L1_conv_B_imag)
    t = _to_tokens(x)
    t = t + _L1_ffn_ref(_ln_t(t), L1_ffn_gate_w, L1_ffn_gate_b, L1_ffn_weight1, L1_ffn_weight2)
    x = _from_tokens(t, x)
    return x


_drawn_inputs = setup_inputs


def setup_inputs(seed=0):
    import zlib

    import numpy as np

    out = dict(_drawn_inputs(seed))
    spreads = {'L0_ffn_gamma': (1.0, 0.55),
     'L0_ffn_beta': (0.0, 0.41),
     'L1_conv_bf': (0.0, 0.8),
     'L1_conv_bi': (0.0, 0.8),
     'L1_conv_bd': (0.0, 0.8),
     'L1_ffn_gate_b': (0.0, 0.1)}
    factors = {'L0_conv_qkv_weight': 7.675,
     'L0_conv_qkv_bias': 8.0,
     'L0_conv_proj_weight': 6.71,
     'L0_conv_proj_bias': 3.193,
     'L0_conv_rel_bias_table': 8.0,
     'L1_conv_Wf': 8.0,
     'L1_conv_Wi': 8.0,
     'L1_conv_Wd': 8.0,
     'L1_conv_A_real': 8.0,
     'L1_conv_A_imag': 8.0,
     'L1_conv_B_real': 8.0,
     'L1_conv_B_imag': 8.0,
     'L1_ffn_gate_w': 8.0,
     'L1_ffn_weight1': 8.0,
     'L1_ffn_weight2': 8.0}
    for name, (base, spread) in spreads.items():
        noise = np.random.default_rng([zlib.crc32(name.encode()), seed]).standard_normal(out[name].shape)
        drawn = base * np.exp(spread * noise) if base else spread * noise
        out[name] = jnp.asarray(drawn.astype(out[name].dtype))
    for name, factor in factors.items():
        out[name] = (out[name] * factor).astype(out[name].dtype)
    return out
```

```python
from contextlib import ExitStack

import numpy as np
import concourse.bass as bass
from concourse import mybir

ALU = mybir.AluOpType
ACT = mybir.ActivationFunctionType
AX = mybir.AxisListType
F32 = mybir.dt.float32
BF16 = mybir.dt.bfloat16

P = 128
C = 128
H = W = 56
S = H * W
T = 2 * W
NT = S // T
GT = 4
NG = NT // GT
WIN = 7
L = WIN * WIN
SHIFT = 3
NW = W // WIN
NH = 4
HD = C // NH
E = 64
HID = 512
OS = 8
TOPK = 8


class Image:

    def __init__(self, idx, half, par):
        self.idx, self.half, self.par = idx, half, par

    def step(self, n):
        idx, par = self.idx + n, (self.par + n) % 2
        half = self.half + (n - par + self.par) // 2
        return Image(idx, half, par)


def wait(eng, sem, value):
    if isinstance(value, int) and value <= 0:
        return
    eng.wait_ge(sem, value)


def rolled(dram_image, tile):
    out = []
    for r in range(2):
        n_wrap = next(n for n in range(NT) if 2 * n + r + SHIFT >= H)
        for n0, n1 in ((0, n_wrap), (n_wrap, NT)):
            h0 = (2 * n0 + r + SHIFT) % H
            for j0, j1 in ((0, W - SHIFT), (W - SHIFT, W)):
                w0 = (j0 + SHIFT) % W
                src = dram_image[h0:h0 + 2 * (n1 - n0 - 1) + 1:2, w0:w0 + j1 - j0, :]
                out.append((src.rearrange("h w c -> w h c"), tile[W * r + j0:W * r + j1, n0:n1, :]))
    return out


PIECES = 8


def moments(dve, halves, mean, var, tmp, sem, base, done):
    dve.tensor_tensor(mean, halves[:, :, 1], halves[:, :, 4], ALU.add)
    dve.tensor_tensor(tmp, halves[:, :, 1], halves[:, :, 4], ALU.subtract)
    dve.tensor_tensor(var, halves[:, :, 2], halves[:, :, 5], ALU.add).then_inc(sem, 1)
    dve.wait_ge(sem, base + 1)
    dve.scalar_tensor_tensor(tmp, tmp, 0.25, tmp, ALU.mult, ALU.mult)
    dve.tensor_scalar(mean, mean, 0.5, None, ALU.mult).then_inc(sem, 1)
    dve.wait_ge(sem, base + 2)
    dve.scalar_tensor_tensor(var, var, 1.0 / C, tmp, ALU.mult, ALU.add).then_inc(done, 1)


def attention_phase(nc, B, x, w_qkvT, qkv_bias, w_projT, proj_bias, rel_table, mask, ident_d, ones_d,
                    x1_d, xh_d, gram):
    with ExitStack() as ctx:
        def sb(name, shape, dt=F32):
            return ctx.enter_context(nc.sbuf_tensor(name, shape, dt))

        def ps(name, shape):
            return ctx.enter_context(nc.psum_tensor(name, shape, F32))

        def sem(name):
            return ctx.enter_context(nc.semaphore(name))

        XL = [sb(f"XL{i}", [T, NT, C]) for i in range(2)]
        XR = [sb(f"XR{i}", [T, NT, C]) for i in range(2)]
        XH = [sb(f"XH{i}", [T, NT, C]) for i in range(2)]
        XT = [sb(f"XT{i}", [C, NW, NW, L]) for i in range(2)]
        OTs = [sb(f"OTs{i}", [C, H, W]) for i in range(2)]
        QT = [sb(f"QT{i}", [C, NW * L + 16]) for i in range(2)]
        KB = [sb(f"KB{i}", [C, NW, NH, L]) for i in range(2)]
        Vb = [sb(f"Vb{i}", [P, NW, 2, 66]) for i in range(2)]
        SS = [sb(f"SS{i}", [P, 16, L]) for i in range(2)]
        PP = [sb(f"PP{i}", [P, 4, NH, 64]) for i in range(2)]
        PT = [sb(f"PT{i}", [P, 4, 2, P]) for i in range(2)]
        On = [sb(f"On{i}", [P, 4, C]) for i in range(2)]
        BT = [sb(f"BT{i}", [P, 4, NH, L]) for i in range(2)]
        mx = [sb(f"mx{i}", [P, 16]) for i in range(2)]
        rc = sb("rc", [P, 2, 4, 2])
        wq = sb("wq", [C, 3 * C])
        wp = sb("wp", [C, C])
        ident = sb("ident", [P, P])
        ones = sb("ones", [P, P])
        qkb = sb("qkb", [C, 3])
        qsb = sb("qsb", [C, 1])
        bvb = sb("bvb", [C, P])
        pbr = sb("pbr", [1, C])
        pbias = sb("pbias", [P, C])
        mk = sb("mk", [P, 4, L])
        rel = sb("rel", [P, NH, L])
        nhalf = sb("nhalf", [T, GT])
        epst = sb("epst", [T, 2, GT])
        st = sb("st", [T, GT, 6])
        mean = [sb(f"mean{i}", [T, GT]) for i in range(2)]
        var = [sb(f"var{i}", [T, GT]) for i in range(2)]
        tmp = sb("tmp", [T, 2, GT])
        rst = [sb(f"rst{i}", [T, GT]) for i in range(2)]
        st2 = sb("st2", [T, GT, 6])
        mean2 = sb("mean2", [T, NG, GT])
        var2 = sb("var2", [T, NG, GT])
        rs2 = sb("rs2", [T, NG, GT])

        pS = ps("pS", [P, 2, 512])
        pO = ps("pO", [P, 2, 512])
        pV = ps("pV", [P, 512])
        pT = ps("pT", [P, 2, 512])
        pX = ps("pX", [P, 512])
        pG = pO[:, 0, 264:264 + C + 1]

        cst = sem("cst"); cst2 = sem("cst2"); ini = sem("ini"); relA = sem("relA")
        relB = sem("relB"); tab = sem("tab"); ctab = sem("ctab"); bvd = sem("bvd"); pbd = sem("pbd")
        pbd2 = sem("pbd2"); zer = sem("zer"); zer2 = sem("zer2"); qsd = sem("qsd")
        xl_ld = [sem(f"xl_ld{i}") for i in range(2)]
        xr_ld = [sem(f"xr_ld{i}") for i in range(2)]
        x1_st = [sem(f"x1_st{i}") for i in range(2)]
        xh_st = [sem(f"xh_st{i}") for i in range(2)]
        st_d = sem("st_d"); mo_d = sem("mo_d"); mo2_d = sem("mo2_d"); ag_d = sem("ag_d"); ep_d = sem("ep_d"); rs_d = sem("rs_d"); xn_d = sem("xn_d")
        xt_ps = sem("xt_ps"); xt_sb = sem("xt_sb")
        q_ps = sem("q_ps"); k_ps = sem("k_ps"); q_sb = sem("q_sb"); k_sb = sem("k_sb")
        s_ps = sem("s_ps"); s_add = sem("s_add"); s_mx = sem("s_mx"); s_sub = sem("s_sub"); p_sb = sem("p_sb")
        pt_ps = sem("pt_ps"); pt_sb = sem("pt_sb")
        v_ps = sem("v_ps"); v_sb = sem("v_sb")
        o_ps = sem("o_ps"); r_sb = sem("r_sb"); on_sb = sem("on_sb")
        ot_ps = sem("ot_ps"); ot_sb = sem("ot_sb")
        xr_b = sem("xr_b"); pj_ps = sem("pj_ps"); x1_sb = sem("x1_sb")
        st2_d = sem("st2_d"); ag2_d = sem("ag2_d"); ep2_d = sem("ep2_d"); rs2_d = sem("rs2_d"); xh_sb = sem("xh_sb")
        g_ps = sem("g_ps"); g_sb = sem("g_sb"); g_z = sem("g_z")
        N_CST = 9

        PROJ = {2: [0, 1], 3: [2, 3], 4: [4], 5: [5], 6: [6]}
        MOM = {s + 1: g for s, g in PROJ.items()}
        UNITS = len(PROJ)

        def bodies(body, eng):
            body(Image(-1, -1, 1), False, False, True)
            body(Image(0, 0, 0), False, True, True)
            body(Image(1, 0, 1), True, True, True)
            if B > 4:
                body(Image(2, 1, 0), True, True, True)
                body(Image(3, 1, 1), True, True, True)
            if B > 6:
                with eng.Fori(0, (B - 6) // 2) as i:
                    body(Image(i * 2 + 4, i + 2, 0), True, True, True)
                    body(Image(i * 2 + 5, i + 2, 1), True, True, True)
            body(Image(B - 2, B // 2 - 1, 0), True, True, True)
            body(Image(B - 1, B // 2 - 1, 1), True, True, False)
            body(Image(B, B // 2, 0), True, False, False)

        block = ctx.enter_context(nc.Block())

        @block.sync
        def _(sp):
            sp.dma_start(wq[:], w_qkvT).then_inc(cst, 16)
            sp.dma_start(wp[:], w_projT).then_inc(cst, 16)
            sp.dma_start(ident[:], ident_d).then_inc(cst, 16)
            sp.dma_start(ones[:], ones_d).then_inc(cst, 16)
            sp.dma_start(qkb[:], qkv_bias.rearrange("(t c) -> c t", t=3), allow_slow_non_contiguous=True).then_inc(cst, 16)
            sp.dma_start(pbr[:], proj_bias.rearrange("(a c) -> a c", a=1)).then_inc(cst, 16)
            sp.dma_start(mk[:], mask).then_inc(cst, 16)
            for b in range(2):
                for src, dst in rolled(x[b], XL[b]):
                    sp.dma_start(dst, src).then_inc(xl_ld[b], 16)

            def body(m, prev, main, nxt):
                if main and (nxt or not isinstance(m.idx, int)) and not (isinstance(m.idx, int) and m.idx + 2 >= B):
                    wait(sp, xt_ps, m.idx * NG + NG)
                    for src, dst in rolled(x[bass.ds(m.idx + 2, 1)].rearrange("a h w c -> (a h) w c"), XL[m.par]):
                        sp.dma_start(dst, src).then_inc(xl_ld[m.par], 16)
                if main:
                    wait(sp, x1_st[m.par], m.half * (16 * PIECES))
                    for src, dst in rolled(x[bass.ds(m.idx, 1)].rearrange("a h w c -> (a h) w c"), XR[m.par]):
                        sp.dma_start(dst, src).then_inc(xr_ld[m.par], 16)
                if prev:
                    q = m.step(-1)
                    wait(sp, x1_sb, m.idx * NG)
                    for dst, src in rolled(x1_d[bass.ds(q.idx, 1)].rearrange("a h w c -> (a h) w c"), XR[q.par]):
                        sp.dma_start(dst, src).then_inc(x1_st[q.par], 16)
                    wait(sp, xh_sb, m.idx * NG)
                    for dst, src in rolled(xh_d[bass.ds(q.idx, 1)].rearrange("a h w c -> (a h) w c"), XH[q.par]):
                        sp.dma_start(dst, src).then_inc(xh_st[q.par], 16)

            bodies(body, sp)
            for i in range(2):
                sp.wait_ge(x1_st[i], B // 2 * 16 * PIECES)
                sp.wait_ge(xh_st[i], B // 2 * 16 * PIECES)

        @block.gpsimd
        def _(pool):
            pool.memset(epst[:, 0, :], 1e-6)
            pool.memset(epst[:, 1, :], 1e-5)
            pool.memset(nhalf[:], -0.5).then_inc(zer2, 1)
            pool.wait_ge(zer2, 1)
            pool.wait_ge(zer, 1)
            for qy in range(WIN):
                for qx in range(WIN):
                    o = (WIN - 1 - qy) * (2 * WIN - 1) + WIN - 1 - qx
                    q = qy * WIN + qx
                    src = bass.AP(tensor=rel_table.tensor, offset=rel_table.offset + o,
                                  ap=[[1, 1], [(2 * WIN - 1) ** 2, NH], [2 * WIN - 1, WIN], [1, WIN]])
                    pool.dma_start(rel[q:q + 1, :, :].rearrange("p h (a b) -> p h a b", a=WIN), src).then_inc(relA, 16)
            pool.wait_ge(relA, 16 * L)
            pool.dma_start(rel[64:64 + L, :, :], rel[0:L, :, :]).then_inc(relB, 16)

            def powers(m, ep_sem, a_sem, r_sem, a, r, base):
                wait(pool, a_sem, base)
                pool.tensor_tensor(r, a, epst[:, m, :], ALU.add).then_inc(ep_sem, 1)
                wait(pool, ep_sem, base)
                pool.tensor_tensor(r, r, nhalf[:, 0:GT], ALU.pow).then_inc(r_sem, 1)

            def body(m, prev, main, nxt):
                n = m.step(1)
                g0 = m.idx * NW
                for wi in range(NW):
                    if nxt and wi < NG:
                        wait(pool, xn_d, n.idx * NG + max(wi - 1, 0))
                        powers(0, ep_d, ag_d, rs_d, var[wi % 2][:], rst[wi % 2][:], n.idx * NG + wi + 1)
                    if main:
                        pool.wait_ge(s_mx, g0 + wi + 1)
                        sv = SS[wi % 2]
                        pool.tensor_tensor(sv[:], sv[:], mx[wi % 2][:].unsqueeze(2).broadcast_to([P, 16, L]),
                                           ALU.subtract).then_inc(s_sub, 1)
                        if wi < NG:
                            if wi == 0:
                                pool.wait_ge(xr_ld[m.par], m.half * (16 * PIECES) + 16 * PIECES)
                                if isinstance(m.idx, int) and m.idx == 0:
                                    pool.wait_ge(pbd2, 1)
                            xr = XR[m.par][:, GT * wi:GT * wi + GT, :]
                            pool.tensor_tensor(xr, xr, pbias[0:T, :].unsqueeze(1).broadcast_to([T, GT, C]),
                                               ALU.add).then_inc(xr_b, 1)
                    if prev and wi in PROJ:
                        for k in PROJ[wi]:
                            b = (m.idx - 1) * NG + k
                            if k < NG:
                                wait(pool, xh_sb, b + 1 - NG)
                            powers(1, ep2_d, ag2_d, rs2_d, var2[:, k, :],
                                   rs2[:, k, :], b + 1)

            bodies(body, pool)

        @block.vector
        def _(dve):
            for i in range(2):
                dve.memset(QT[i][:], 0.0)
                dve.memset(KB[i][:], 0.0)
                dve.memset(PP[i][:], 0.0)
                dve.memset(Vb[i][:], 0.0).then_inc(ini, 1)
            dve.memset(gram[:], 0.0).then_inc(g_z, 1)
            dve.memset(rel[:], 0.0).then_inc(zer, 1)
            dve.wait_ge(ini, 2)
            for i in range(2):
                dve.memset(Vb[i][0:64, :, :, 64:65], 1.0)
                dve.memset(Vb[i][64:P, :, :, 65:66], 1.0).then_inc(ini, 1)
            dve.wait_ge(cst, 16 * 7)
            dve.tensor_scalar(qsb[:], qkb[:, 0:1], float(HD) ** -0.5, None, ALU.mult).then_inc(qsd, 1)
            dve.tensor_copy(bvb[:], qkb[:, 2:3].broadcast_to([C, P])).then_inc(bvd, 1)
            dve.wait_ge(pbd, 1)
            dve.tensor_copy(pbias[:], pV[:, 0:C]).then_inc(pbd2, 1)
            dve.wait_ge(relB, 16)
            for last in range(2):
                for p in range(4):
                    mm = mk[:, 2 * last + (p == 3), :].unsqueeze(1).broadcast_to([P, NH, L])
                    dve.tensor_tensor(BT[last][:, p, :, :], rel[:], mm, ALU.add).then_inc(tab, 1)

            def stats(xv, s_, m_, v_, t_, s_sem, mo_sem, a_sem, base):
                wait(dve, a_sem, base - 1)
                for t in range(GT):
                    i = dve.bn_stats(s_[:, t, :], xv[:, t, :])
                i.then_inc(s_sem, 1)
                wait(dve, s_sem, base)
                moments(dve, s_, m_, v_, t_, mo_sem, (base - 1) * 2, a_sem)

            def body(m, prev, main, nxt):
                n, q = m.step(1), m.step(-1)
                g0 = m.idx * NW
                for wi in range(NW):
                    g = g0 + wi
                    if nxt and wi < NG:
                        if wi == 0:
                            dve.wait_ge(xl_ld[n.par], n.half * (16 * PIECES) + 16 * PIECES)
                        wait(dve, rs_d, n.idx * NG + max(wi - 1, 0))
                        wait(dve, xn_d, n.idx * NG + max(wi - 1, 0))
                        stats(XL[n.par][:, GT * wi:GT * wi + GT, :], st, mean[wi % 2][:], var[wi % 2][:],
                              tmp[:, 0, :], st_d, mo_d, ag_d, n.idx * NG + wi + 1)
                    if nxt and wi >= 1:
                        k = wi - 1
                        dve.wait_ge(rs_d, n.idx * NG + k + 1)
                        for t in range(GT):
                            xv = XL[n.par][:, GT * k + t, :]
                            i = dve.tensor_scalar(xv, xv, mean[k % 2][:, t:t + 1], rst[k % 2][:, t:t + 1],
                                                  ALU.subtract, ALU.mult)
                        i.then_inc(xn_d, 1)
                    if main:
                        dve.wait_ge(s_ps, g + 1)
                        wait(dve, p_sb, g - 1)
                        if isinstance(m.idx, int) and g == 0:
                            dve.wait_ge(tab, 8)
                        dve.tensor_tensor(SS[wi % 2][:].rearrange("p (a b) l -> p a (b l)", a=2), pS[:, :, 0:8 * L],
                                          BT[wi == NW - 1][:].rearrange("p (a b) h l -> p a (b h l)", a=2),
                                          ALU.add).then_inc(s_add, 1)
                        dve.wait_ge(s_add, g + 1)
                        dve.tensor_reduce(mx[wi % 2][:], SS[wi % 2][:], AX.X, ALU.max).then_inc(s_mx, 1)
                        dve.wait_ge(v_ps, g + 1)
                        wait(dve, o_ps, g - 1)
                        for o in range(2):
                            i = dve.tensor_copy(Vb[wi % 2][64 * o:64 * o + L, :, :, HD * o:HD * o + HD],
                                                pV[64 * o:64 * o + L, :].rearrange("p (w a d) -> p w a d", w=NW, a=2))
                        i.then_inc(v_sb, 1)
                    if main and not (isinstance(m.idx, int) and g == 0) or (prev and wi == 0):
                        dve.wait_ge(o_ps, g)
                        wait(dve, on_sb, g - 1)
                        dve.reciprocal(rc[:], pO[:, :, 0:264].rearrange("p a (w e) -> p a w e", e=66)[:, :, :, 64:66]
                                       ).then_inc(r_sb, 1)
                        dve.wait_ge(r_sb, g)
                        wait(dve, ot_ps, g - 2)
                        for hp in range(2):
                            i = dve.tensor_tensor(
                                On[(wi + 1) % 2][:, :, 64 * hp:64 * hp + 64].rearrange("p w (h d) -> p w h d", h=2),
                                pO[:, hp, 0:264].rearrange("p (w e) -> p w e", e=66)[:, :, 0:64]
                                .rearrange("p w (h d) -> p w h d", h=2),
                                rc[:, hp, :, :].unsqueeze(3).broadcast_to([P, 4, 2, HD]), ALU.mult)
                        i.then_inc(on_sb, 1)
                    if prev and wi in PROJ:
                        for k in PROJ[wi]:
                            b = q.idx * NG + k
                            dve.wait_ge(pj_ps, b + 1)
                            dve.wait_ge(xr_b, b + 1)
                            xv = XR[q.par][:, GT * k:GT * k + GT, :]
                            dve.tensor_tensor(xv, pT[0:T, 1, :].rearrange("p (t c) -> p t c", t=GT), xv,
                                              ALU.add).then_inc(x1_sb, 1)
                            dve.wait_ge(x1_sb, b + 1)
                            wait(dve, rs2_d, b + 1 - NG)
                            wait(dve, xh_sb, b + 1 - NG)
                            stats(xv, st2, mean2[:, k, :], var2[:, k, :], tmp[:, 1, :], st2_d, mo2_d, ag2_d, b + 1)
                    if prev and wi in MOM:
                        for k in MOM[wi]:
                            b = q.idx * NG + k
                            dve.wait_ge(rs2_d, b + 1)
                            if k == 0:
                                wait(dve, xh_st[q.par], q.half * (16 * PIECES))
                                wait(dve, g_ps, (q.idx - 1) * UNITS)
                            for t in range(GT):
                                i = dve.tensor_scalar(XH[q.par][:, GT * k + t, :], XR[q.par][:, GT * k + t, :],
                                                      mean2[:, k, t:t + 1], rs2[:, k, t:t + 1],
                                                      ALU.subtract, ALU.mult)
                            i.then_inc(xh_sb, 1)
                        u = q.idx * UNITS + list(MOM).index(wi)
                        dve.wait_ge(g_ps, u + 1)
                        wait(dve, g_sb, u)
                        dve.tensor_tensor(gram[:], gram[:], pG, ALU.add).then_inc(g_sb, 1)

            dve.wait_ge(g_z, 1)
            bodies(body, dve)

        @block.scalar
        def _(act):
            act.wait_ge(qsd, 1)
            act.wait_ge(ini, 4)

            def turn(n, k):
                act.wait_ge(xt_ps, n.idx * NG + k + 1)
                wait(act, v_ps, (n.idx - 1) * NW)
                r0, r1 = 2 * GT * k, 2 * GT * (k + 1)
                for i0, i1 in ((r0, (r0 // WIN + 1) * WIN), ((r0 // WIN + 1) * WIN, r1)):
                    if i1 > i0:
                        src = pX[:, W * (i0 - r0):W * (i1 - r0)].rearrange("c (r w k) -> c w r k", w=NW, k=WIN)
                        dst = XT[n.par][:, i0 // WIN, :, :].rearrange("c w (r k) -> c w r k", r=WIN)
                        i = act.copy(dst[:, :, i0 % WIN:i0 % WIN + i1 - i0, :], src)
                i.then_inc(xt_sb, 1)

            def evacuate_qk(g, par):
                act.wait_ge(q_ps, g + 1)
                wait(act, s_ps, g - 1)
                act.activation(QT[par][:, 0:NW * L], pX[:, 0:NW * L], ACT.Identity, bias=qsb[:, 0:1],
                               scale=float(HD) ** -0.5).then_inc(q_sb, 1)
                act.wait_ge(k_ps, g + 1)
                for h in range(NH):
                    r = slice(HD * h, HD * h + HD)
                    i = act.activation(KB[par][r, :, h, :], pV[r, 0:NW * L].rearrange("c (w l) -> c w l", l=L),
                                       ACT.Identity, bias=qkb[r, 1:2])
                i.then_inc(k_sb, 1)

            def body(m, prev, main, nxt):
                n, q = m.step(1), m.step(-1)
                g0 = m.idx * NW
                for wi in range(NW):
                    g = g0 + wi
                    if main and wi + 1 < NW:
                        evacuate_qk(g + 1, (wi + 1) % 2)
                    elif wi == NW - 1 and nxt and main:
                        evacuate_qk(g + 1, 0)
                    if main and not (isinstance(m.idx, int) and g == 0) or (prev and wi == 0):
                        wait(act, o_ps, g - 2)
                        for a in range(2):
                            act.wait_ge(pt_ps, g * 2 - 1 + a)
                            act.copy(PT[(wi + 1) % 2][:, 2 * a:2 * a + 2, :, :].rearrange("p a b c -> p (a b c)"),
                                     pT[:, a, :]).then_inc(pt_sb, 1)
                    if nxt and wi >= 1:
                        turn(n, wi - 1)
                    if (main and not (isinstance(m.idx, int) and g < 2)) or (prev and wi < 2):
                        act.wait_ge(ot_ps, g - 1)
                        im, row = (q, NW - 2 + wi) if wi < 2 else (m, wi - 2)
                        wait(act, pj_ps, (im.idx - 1) * NG)
                        act.copy(OTs[im.par][:, WIN * row:WIN * row + WIN, :].rearrange("c r (w k) -> c w r k", w=NW),
                                 pT[:, 0, :].rearrange("c (w e) -> c w e", w=NW)[:, :, 0:L]
                                 .rearrange("c w (r k) -> c w r k", r=WIN)).then_inc(ot_sb, 1)
                    if main:
                        act.wait_ge(s_sub, g + 1)
                        wait(act, pt_ps, g * 2 - 2)
                        act.activation(PP[wi % 2][:].rearrange("p w h k -> p (w h) k")[:, :, 0:L], SS[wi % 2][:],
                                       ACT.Exp).then_inc(p_sb, 1)
                if nxt and not main:
                    evacuate_qk(0, 0)

            bodies(body, act)

        @block.tensor
        def _(pe):
            pe.wait_ge(cst, 16 * 7)
            pe.wait_ge(bvd, 1)
            pe.matmul(pV[:, 0:C], bvb[:], wp[:], start=True, stop=False)
            pe.matmul(pV[:, 0:C], ones[0:1, :], pbr[:], start=False, stop=True).then_inc(pbd, 1)
            pe.wait_ge(pbd2, 1)

            def windows(im, wi):
                return XT[im.par][:, wi, :, :].rearrange("c w l -> c (w l)")

            def qk(im, wi, g, g_main=True):
                if wi != 2:
                    turned = im.idx * NG + (NG - 1 if wi == 0 and g_main else NG + max(wi - 2, 0))
                    pe.wait_ge(xt_sb, min(turned, B * NG) if isinstance(turned, int) else turned)
                wait(pe, q_sb, g)
                out = pX[:, 0:NW * L]
                pe.matmul(out, wq[:, 0:C], windows(im, wi), start=True, stop=True).then_inc(q_ps, 1)
                wait(pe, v_sb, g - 1)
                wait(pe, k_sb, g)
                out = pV[:, 0:NW * L]
                pe.matmul(out, wq[:, C:2 * C], windows(im, wi), start=True, stop=True).then_inc(k_ps, 1)

            def scores(g, par):
                pe.wait_ge(q_sb, g + 1)
                pe.wait_ge(k_sb, g + 1)
                wait(pe, s_add, g)
                for w in range(NW):
                    p, s = w // 2, w % 2
                    i = pe.matmul(pS[64 * s:64 * s + 64, p // 2, (p % 2) * NH * L:(p % 2 + 1) * NH * L],
                                  QT[par][:, w * L:w * L + 64], KB[par][:, w, :, :].rearrange("c h k -> c (h k)"),
                                  start=True, stop=True)
                i.then_inc(s_ps, 1)

            def turn_probs(g, par):
                pe.wait_ge(p_sb, g + 1)
                wait(pe, ot_sb, g - 1)
                for a in range(2):
                    for p in range(2):
                        for hp in range(2):
                            i = pe.transpose(pT[:, a, (2 * p + hp) * P:(2 * p + hp + 1) * P],
                                             PP[par][:, 2 * a + p, 2 * hp:2 * hp + 2, :].rearrange("p h k -> p (h k)"),
                                             ident[:])
                    i.then_inc(pt_ps, 1)

            def values(im, wi, g, k_issued):
                if k_issued:
                    pe.wait_ge(k_sb, g + 2)
                wait(pe, v_sb, g)
                for w in range(NW):
                    for o in range(2):
                        i = pe.matmul(pV[64 * o:64 * o + L, 64 * w:64 * w + 64],
                                      XT[im.par][:, wi, w, :],
                                      wq[:, 2 * C:3 * C].rearrange("c (a b d) -> c a b d", a=2, b=2)[:, :, o, :],
                                      start=True, stop=True)
                i.then_inc(v_ps, 1)

            def turn_x(n, k, g):
                pe.wait_ge(xn_d, n.idx * NG + k + 1)
                wait(pe, xt_sb, n.idx * NG + k)
                wait(pe, q_sb, g)
                for t in range(GT):
                    i = pe.transpose(pX[:, T * t:T * t + T], XL[n.par][:, GT * k + t, :], ident[0:T, 0:T])
                i.then_inc(xt_ps, 1)

            def weigh(g, par):
                pe.wait_ge(pt_sb, g * 2 + 2)
                pe.wait_ge(v_sb, g + 1)
                wait(pe, on_sb, g)
                for hp in range(2):
                    for w in range(NW):
                        p, s = w // 2, w % 2
                        i = pe.matmul(pO[64 * s:64 * s + 64, hp, 66 * p:66 * p + 66],
                                      PT[par][:, p, hp, 64 * s:64 * s + 64], Vb[par][:, w, hp, :],
                                      start=True, stop=True)
                i.then_inc(o_ps, 1)

            def turn_out(g, par, last_pt):
                pe.wait_ge(on_sb, g + 1)
                wait(pe, pt_sb, last_pt)
                wait(pe, ot_sb, g)
                for p in range(4):
                    i = pe.transpose(pT[:, 0, P * p:P * p + P], On[par][:, p, :], ident[:])
                i.then_inc(ot_ps, 1)

            def body(m, prev, main, nxt):
                n, q = m.step(1), m.step(-1)
                g0 = m.idx * NW
                for wi in range(NW):
                    g = g0 + wi
                    k_issued = main and (wi + 1 < NW or nxt)
                    if main and wi + 1 < NW:
                        qk(m, wi + 1, g + 1)
                    elif main and nxt:
                        qk(n, 0, g + 1)
                    if main:
                        scores(g, wi % 2)
                    first = isinstance(m.idx, int) and m.idx == 0
                    older = (main and not (first and wi == 0)) or (prev and wi == 0)
                    if older:
                        done = (m.idx - 1) * NG + (0 if wi < 3 else PROJ[min(wi - 1, 6)][-1] + 1)
                        wait(pe, x1_sb, done)
                        turn_probs(g - 1, (wi + 1) % 2)
                    if main:
                        values(m, wi, g, k_issued)
                    if nxt and wi >= 1:
                        turn_x(n, wi - 1, g + 2 if main else 0)
                    if older:
                        wait(pe, g_sb, (m.idx - 1) * UNITS + sum(s < wi for s in MOM))
                        weigh(g - 1, (wi + 1) % 2)
                    if (main and not (first and wi < 2)) or (prev and wi < 2):
                        turn_out(g - 2, wi % 2, g * 2 if main else g0 * 2)
                    if prev and wi in PROJ:
                        for j, k in enumerate(PROJ[wi]):
                            b = q.idx * NG + k
                            if j == 0:
                                if wi == 2:
                                    pe.wait_ge(ot_sb, m.idx * NW)
                                pe.wait_ge(pt_sb, (g if main else g0) * 2)
                            wait(pe, x1_sb, b)
                            for t in range(GT):
                                n0 = GT * k + t
                                i = pe.matmul(pT[0:T, 1, C * t:C * t + C],
                                              OTs[q.par][:, 2 * n0:2 * n0 + 2, :].rearrange("c a b -> c (a b)"), wp[:],
                                              start=True, stop=True)
                            i.then_inc(pj_ps, 1)
                    if prev and wi in MOM:
                        pe.wait_ge(xh_sb, q.idx * NG + MOM[wi][-1] + 1)
                        u = q.idx * UNITS + list(MOM).index(wi)
                        wait(pe, g_sb, u)
                        wait(pe, on_sb, g if main else g0)
                        tiles = [GT * k + t for k in MOM[wi] for t in range(GT)]
                        for t in tiles:
                            pe.matmul(pG[:, 0:C], XH[q.par][:, t, :], XH[q.par][:, t, :], start=t == tiles[0],
                                      stop=t == tiles[-1], skip_group_check=True)
                            i = pe.matmul(pG[:, C:C + 1], XH[q.par][:, t, :], ones[0:T, 0:1], start=False,
                                          stop=t == tiles[-1], skip_group_check=True)
                        i.then_inc(g_ps, 1)
                if nxt and not main:
                    qk(n, 0, 0, False)

            bodies(body, pe)


def scan_phase(nc, B, x1_d, xh_d, gram, w_ffnT, v_ffnT, gamma, beta, w_gates, b_gates, dft, kernA, kernB,
               ident_d, ones_d, x3_d):
    NO = B // OS
    SLOTS = 8
    NX = 3
    K = T // SLOTS
    R = K // 2
    N = B * S
    Q = OS // 2
    HC = C // 2
    with ExitStack() as ctx:
        def sb(name, shape, dt=F32):
            return ctx.enter_context(nc.sbuf_tensor("s_" + name, shape, dt))

        def ps(name, shape):
            return ctx.enter_context(nc.psum_tensor("s_" + name, shape, F32))

        def sem(name):
            return ctx.enter_context(nc.semaphore("s_" + name))

        XT = [sb(f"XT{i}", [C, B, T]) for i in range(2)]
        U = [sb(f"U{i}", [C, T, B]) for i in range(2)]
        XQ = [sb(f"XQ{i}", [T, Q, C]) for i in range(2)]
        X2 = [sb(f"X2{i}", [T, OS, C]) for i in range(NX)]
        XN = sb("XN", [T, OS, C])
        XNT = sb("XNT", [C, OS, T])
        TG = [sb(f"TG{i}", [T, OS, 2 * C]) for i in range(2)]
        Z = sb("Z", [T, OS, C])
        Dl = sb("Dl", [T, OS, C])
        BX = sb("BX", [T, OS, C])
        W2 = sb("W2", [T, OS, C])
        Wv = sb("Wv", [T, OS, C])
        IN = sb("IN", [T, OS, C])
        half = {n: sb(n, [T, OS, HC]) for n in ("t0", "d0", "t1", "d1", "t2", "d2", "q0", "q1", "q2")}
        par_a = [sb(f"par_a{i}", [T, 5 * HC]) for i in range(2)]
        par_b = [sb(f"par_b{i}", [T, 4 * HC]) for i in range(2)]
        raw = sb("raw", [T, 4 * HC])
        sa = sb("sa", [T, HC])
        sc_ = sb("sc_", [T, HC])
        phalf = sb("phalf", [T, HC])
        nhalf = sb("nhalf", [P, C])
        epst = sb("epst", [T, OS])
        eps8 = sb("eps8", [T, HC])
        D = sb("D", [P, T])
        kern = sb("kern", [P, 4 * HC])
        wg = sb("wg", [C, 3 * C])
        b3 = sb("b3", [3, 3 * C], BF16)
        ones3 = sb("ones3", [3, T], BF16)
        ws = sb("ws", [C, C])
        vh = sb("vh", [C, C])
        zb = sb("zb", [C, 1])
        ident = sb("ident", [P, P])
        st = sb("st", [T, OS, 6])
        mean = sb("mean", [T, OS])
        var = sb("var", [T, OS])
        tmp = sb("tmp", [T, OS])
        twentieth = sb("twentieth", [T, HC])
        rst = sb("rst", [T, OS])
        cols = sb("cols", [P, 2])
        pW = [ps(f"pW{i}", [C, 512]) for i in range(2)]
        pX = ps("pX", [P, 512])
        pY = ps("pY", [P, 512])
        pN = ps("pN", [P, 512])
        pG = [ps(f"pG{i}", [P, 512]) for i in range(3)]

        cst = sem("cst"); ini = sem("ini"); dch = sem("dch"); pch = sem("pch"); mmc = sem("mmc")
        b3d = sem("b3d"); bres_d = sem("bres_d"); ready = sem("ready"); splt = sem("splt")
        xq_ld = [sem(f"xq_ld{i}") for i in range(2)]
        x2_ld = [sem(f"x2_ld{i}") for i in range(NX)]
        x3_st = sem("x3_st")
        d_ld = sem("d_ld"); d_ps = sem("d_ps")
        xt_ps = sem("xt_ps"); xt_sb = sem("xt_sb")
        w_ps = sem("w_ps"); z_ps = sem("z_ps"); u_sb = sem("u_sb")
        y_ps = sem("y_ps"); x2_d = sem("x2_d"); st_d = sem("st_d"); mo_d = sem("mo_d"); ag_d = sem("ag_d"); ep_d = sem("ep_d")
        rs_d = sem("rs_d"); xn_d = sem("xn_d"); n_ps = sem("n_ps"); n_sb = sem("n_sb")
        g_ps = sem("g_ps"); g_sb = sem("g_sb"); sp_d = sem("sp_d")
        raw_d = sem("raw_d"); pr_d = sem("pr_d"); mag_d = sem("mag_d"); th_d = sem("th_d"); pa_d = sem("pa_d")
        pb_d = sem("pb_d"); pm_d = sem("pm_d")
        bp = sem("bp"); bx_d = sem("bx_d"); wp_d = sem("wp_d"); wv_d = sem("wv_d")
        dv = sem("dv"); am = sem("am")
        NV = 28
        NA = 8

        brow = Z[0:1, :, :].rearrange("p a b -> p (a b)")[:, 0:3 * C]
        bres = Wv[0:1, :, :].rearrange("p a b -> p (a b)")[:, 0:6 * C].rearrange("p (a b) -> p a b", a=2)
        bhi = W2[0:1, :, :].rearrange("p a b -> p (a b)")[:, 0:9 * HC].bitcast(BF16).rearrange("p (a b) -> p a b", a=3)
        block = ctx.enter_context(nc.Block())

        wt = XNT[:].rearrange("p a b -> p (a b)")[:, 0:C]
        vt = XNT[:].rearrange("p a b -> p (a b)")[:, C:2 * C]
        onesm = XNT[:].rearrange("p a b -> p (a b)")[:, 2 * C:3 * C]
        gam = XNT[:].rearrange("p a b -> p (a b)")[:, 3 * C:4 * C]
        bet = XNT[:].rearrange("p a b -> p (a b)")[:, 4 * C:5 * C]
        mb = XNT[:].rearrange("p a b -> p (a b)")[:, 5 * C:6 * C]
        ee = XNT[:].rearrange("p a b -> p (a b)")[:, 6 * C:7 * C]
        fld = [U[0][:].rearrange("p a b -> p (a b)")[:, i * C:i * C + C] for i in range(6)]

        def chunks(body, eng):
            body(Image(-1, -1, 1), True, False, False, False)
            body(Image(0, 0, 0), True, True, False, False)
            body(Image(1, 0, 1), True, True, True, False)
            body(Image(2, 1, 0), True, True, True, True)
            body(Image(3, 1, 1), True, True, True, True)
            with eng.Fori(0, (NT - 6) // 2) as i:
                body(Image(i * 2 + 4, i + 2, 0), True, True, True, True)
                body(Image(i * 2 + 5, i + 2, 1), True, True, True, True)
            body(Image(NT - 2, NT // 2 - 1, 0), True, True, True, True)
            body(Image(NT - 1, NT // 2 - 1, 1), False, True, True, True)
            body(Image(NT, NT // 2, 0), False, False, True, True)
            body(Image(NT + 1, NT // 2, 1), False, False, False, True)

        def math_octet(j, s, conv, late):
            if s == 0:
                return ((j.idx - 1) * NO - 1, 1, j.par, late and NO == SLOTS)
            return ((j.idx - 1) * NO + s - 1, (s - 1) % 2, (j.par + 1) % 2, conv and s <= NO)

        @block.sync
        def _(sp):
            for dst, src in ((wg[:], w_gates), (ident[:], ident_d), (wt, w_ffnT), (vt, v_ffnT), (onesm, ones_d),
                             (gam, gamma.rearrange("(a c) -> a c", a=1).broadcast_to([P, C])),
                             (bet, beta.rearrange("(a c) -> a c", a=1).broadcast_to([P, C])),
                             (brow, b_gates.rearrange("(a c) -> a c", a=1))):
                sp.dma_start(dst, src).then_inc(cst, 16)
            sp.wait_ge(ini, 1)
            for i, kd in enumerate((kernA, kernB)):
                re, im = kd[0], kd[1]
                o = 2 * HC * i
                sp.dma_start(kern[0:L, o:o + HC], re).then_inc(cst, 16)
                sp.dma_start(kern[0:L, o + HC:o + 2 * HC], im).then_inc(cst, 16)
                sp.dma_start(kern[64:64 + L, o:o + HC], im).then_inc(cst, 16)
                sp.dma_start(kern[64:64 + L, o + HC:o + 2 * HC], re).then_inc(cst, 16)
            sp.wait_ge(splt, 5)
            for i in range(3):
                sp.dma_start(b3[i:i + 1, :], bhi[:, i, :]).then_inc(b3d, 16)

            def tokens(dram, b0, n, c):
                return dram[b0:b0 + n, bass.ds(c * T, T), :].rearrange("b t c -> t b c")

            def load_x1(c, s):
                if s:
                    last = s - NX if s >= NX else max(x for x in range(NO) if x % NX == s % NX) - NO
                    wait(sp, dv, (c.idx * NO + last + 1) * NV)
                sp.dma_start(X2[s % NX][:], tokens(x1_d, OS * s, OS, c.idx)).then_inc(x2_ld[s % NX], 16)

            def body(j, prep, scan, conv, late):
                n, c = j.step(1), j.step(-1)
                for s in range(SLOTS):
                    if prep and s < NO:
                        for a in range(2):
                            o = n.idx * NO + s
                            wait(sp, xt_ps, o * 2 + a - 1)
                            sp.dma_start(XQ[a][:], tokens(xh_d, OS * s + Q * a, Q, n.idx)).then_inc(xq_ld[a], 16)
                    if conv and s + 1 < NO:
                        load_x1(c, s + 1)
                    o, par, cpar, there = math_octet(j, s, conv, late)
                    if there:
                        sp.wait_ge(dv, o * NV + NV)
                    if scan and s == 1:
                        sp.dma_start(D[:], dft[bass.ds(j.idx, 1), :, :].rearrange("a p t -> p (a t)")).then_inc(d_ld, 16)
                    if there:
                        t_, b_ = (c.idx * T - T, OS * (NO - 1)) if s == 0 else (c.idx * T, OS * (s - 1))
                        sp.dma_start(x3_d[b_:b_ + OS, bass.ds(t_, T), :].rearrange("b t c -> t b c"),
                                     Wv[:]).then_inc(x3_st, 16)
                    if scan and s == SLOTS - 1:
                        load_x1(j, 0)

            chunks(body, sp)
            sp.wait_ge(x3_st, NT * NO * 16)

        @block.gpsimd
        def _(pool):
            pool.memset(kern[:], 0.0).then_inc(ini, 1)
            pool.memset(nhalf[:], -0.5)
            pool.memset(epst[:], 1e-6)
            pool.memset(twentieth[:], 0.05)
            pool.memset(eps8[:], 1e-8)
            pool.memset(phalf[:], 0.5)
            pool.memset(ones3[:], 1.0)
            pool.memset(cols[:, 0:1], 1.0)
            pool.memset(cols[:, 1:2], 0.5).then_inc(pch, 1)
            pool.wait_ge(pch, 1)
            pool.wait_ge(dch, 5)
            pool.tensor_tensor(fld[4], fld[3], nhalf[:, 0:C], ALU.pow).then_inc(pch, 1)
            pool.wait_ge(b3d, 48)

            def body(j, prep, scan, conv, late):
                c = j.step(-1)
                for s in range(SLOTS):
                    if scan and s == SLOTS - 2:
                        pool.wait_ge(raw_d, j.idx + 1)
                        wait(pool, bx_d, (j.idx - 1) * NO)
                        pb = par_b[j.par]
                        pool.tensor_tensor(pb[:, 0:HC], raw[:, 2 * HC:3 * HC], twentieth[:], ALU.mult)
                        pool.tensor_scalar(pb[:, HC:2 * HC], raw[:, 2 * HC:3 * HC], 0.05, None, ALU.mult)
                        pool.tensor_scalar(pb[:, 2 * HC:3 * HC], raw[:, 3 * HC:4 * HC], -0.05, None, ALU.mult)
                        pool.tensor_scalar(pb[:, 3 * HC:4 * HC], raw[:, 3 * HC:4 * HC], 0.05, None,
                                           ALU.mult).then_inc(pb_d, 1)
                        pool.wait_ge(pr_d, j.idx * 3 + 3)
                        pool.tensor_tensor(sa[:], sa[:], eps8[:], ALU.add).then_inc(pm_d, 1)
                        pool.wait_ge(pm_d, j.idx + 1)
                        pool.tensor_tensor(sa[:], sa[:], phalf[:], ALU.pow).then_inc(mag_d, 1)
                    if conv and s < NO:
                        o = c.idx * NO + s
                        pool.wait_ge(ag_d, o + 1)
                        wait(pool, xn_d, o)
                        pool.tensor_tensor(rst[:], var[:], epst[:, 0:OS], ALU.add).then_inc(ep_d, 1)
                        pool.wait_ge(ep_d, o + 1)
                        pool.tensor_tensor(rst[:], rst[:], nhalf[0:T, 0:OS], ALU.pow).then_inc(rs_d, 1)
                    o, par, cpar, there = math_octet(j, s, conv, late)
                    if there:
                        pool.wait_ge(dv, o * NV + 7)
                        wait(pool, bx_d, o + 1)
                        wait(pool, x3_st, o * 16)
                        if s == 1:
                            pool.wait_ge(pa_d, c.idx * 8 + 8)
                        a = par_a[cpar]
                        pool.tensor_tensor(Wv[:], IN[:], a[:, 0:C].unsqueeze(1).broadcast_to([T, OS, C]), ALU.mult)
                        for r in range(2):
                            w = pool.tensor_tensor(W2[:, :, HC * r:HC * r + HC], IN[:, :, HC * (1 - r):HC * (1 - r) + HC],
                                                   a[:, C + HC * r:C + HC * r + HC].unsqueeze(1).broadcast_to([T, OS, HC]),
                                                   ALU.mult)
                        w.then_inc(wp_d, 1)
                        pool.wait_ge(wp_d, o + 1)
                        pool.tensor_tensor(Wv[:], Wv[:], W2[:], ALU.add).then_inc(wv_d, 1)
                    if conv and s < NO:
                        o = c.idx * NO + s
                        pool.wait_ge(xn_d, o + 1)
                        wait(pool, dv, o * NV - NV + 7)
                        wait(pool, wv_d, o)
                        b = par_b[c.par]
                        if s == 0:
                            pool.wait_ge(pb_d, c.idx + 1)
                        pool.tensor_tensor(BX[:], XN[:], b[:, 0:C].unsqueeze(1).broadcast_to([T, OS, C]), ALU.mult)
                        for r in range(2):
                            w = pool.tensor_tensor(W2[:, :, HC * r:HC * r + HC], XN[:, :, HC * (1 - r):HC * (1 - r) + HC],
                                                   b[:, C + HC * r:C + HC * r + HC].unsqueeze(1).broadcast_to([T, OS, HC]),
                                                   ALU.mult)
                        w.then_inc(bp, 1)
                        pool.wait_ge(bp, o + 1)
                        pool.tensor_tensor(BX[:], BX[:], W2[:], ALU.add).then_inc(bx_d, 1)

            chunks(body, pool)

        @block.vector
        def _(dve):
            dve.wait_ge(cst, 16 * 16)
            dve.tensor_scalar(brow[:, 0:C], brow[:, 0:C], 2.0, None, ALU.add).then_inc(splt, 1)
            dve.wait_ge(splt, 1)
            dve.tensor_copy(bhi[:, 0, :], brow).then_inc(splt, 1)
            dve.wait_ge(splt, 2)
            dve.tensor_tensor(bres[:, 0, :], brow, bhi[:, 0, :], ALU.subtract).then_inc(bres_d, 1)
            dve.wait_ge(bres_d, 1)
            dve.tensor_copy(bhi[:, 1, :], bres[:, 0, :]).then_inc(splt, 1)
            dve.wait_ge(splt, 3)
            dve.tensor_tensor(bres[:, 1, :], bres[:, 0, :], bhi[:, 1, :], ALU.subtract).then_inc(splt, 1)
            dve.wait_ge(splt, 4)
            dve.tensor_copy(bhi[:, 2, :], bres[:, 1, :]).then_inc(splt, 1)
            for i in range(2):
                o = 2 * HC * i + HC
                w = dve.tensor_scalar(kern[64:P, o:o + HC], kern[64:P, o:o + HC], -1.0, None, ALU.mult)
            w.then_inc(ready, 1)
            dve.tensor_scalar(mb, gram[:, C:C + 1].broadcast_to([P, C]), 1.0 / N, None, ALU.mult).then_inc(dch, 1)
            dve.wait_ge(mmc, 1)
            dve.scalar_tensor_tensor(ee, pG[0][:, 0:C], 1.0 / N, wt, ALU.mult, ALU.mult).then_inc(dch, 1)
            dve.wait_ge(mmc, 2)
            dve.tensor_copy(fld[0], pG[1][:, 0:C]).then_inc(dch, 1)
            dve.wait_ge(dch, 3)
            dve.tensor_tensor(fld[1], fld[0], fld[0], ALU.mult).then_inc(dch, 1)
            dve.wait_ge(dch, 4)
            dve.wait_ge(mmc, 3)
            dve.scalar_tensor_tensor(fld[3], pG[2][:, 0:C], 1e-5, fld[1], ALU.add, ALU.subtract).then_inc(dch, 1)
            dve.wait_ge(pch, 2)
            dve.tensor_tensor(fld[4], fld[4], gam, ALU.mult).then_inc(dch, 1)
            dve.wait_ge(dch, 6)
            dve.tensor_tensor(ws[:], wt, fld[4], ALU.mult).then_inc(dch, 1)
            dve.tensor_tensor(fld[0], fld[0], fld[4], ALU.mult).then_inc(dch, 1)
            dve.tensor_scalar(vh[:], vt, 0.5, None, ALU.mult).then_inc(dch, 1)
            dve.wait_ge(dch, 9)
            dve.tensor_tensor(fld[0], bet, fld[0], ALU.subtract).then_inc(dch, 1)
            dve.wait_ge(dch, 10)
            dve.wait_ge(mmc, 4)
            dve.tensor_tensor(fld[0], fld[0], pW[0][:, 0:C], ALU.add).then_inc(dch, 1)
            dve.wait_ge(dch, 11)
            dve.tensor_tensor(fld[0], fld[0], ident[:], ALU.mult).then_inc(dch, 1)
            dve.wait_ge(dch, 12)
            dve.tensor_reduce(zb[:], fld[0], AX.X, ALU.add).then_inc(dch, 1)
            dve.wait_ge(dch, 13)
            dve.tensor_scalar(zb[:], zb[:], 0.5, None, ALU.mult).then_inc(dch, 1)
            dve.memset(U[1][:, T - 1, :], -1.0).then_inc(ready, 1)

            t0, d0, t1, d1, t2, d2, q0, q1, q2, c1, c2 = (half[n][:] for n in (
                "t0", "d0", "t1", "d1", "t2", "d2", "q0", "q1", "q2", "q2", "t2"))

            def body(j, prep, scan, conv, late):
                c = j.step(-1)
                for s in range(SLOTS):
                    if scan and s == SLOTS - 2:
                        dve.wait_ge(d_ps, j.idx + 1)
                        wait(dve, pa_d, j.idx * 8)
                        wait(dve, pb_d, j.idx)
                        dve.tensor_copy(raw[:], pN[0:T, 0:4 * HC]).then_inc(raw_d, 1)
                        dve.wait_ge(raw_d, j.idx + 1)
                        dve.tensor_tensor(sa[:], raw[:, 0:HC], raw[:, 0:HC], ALU.mult).then_inc(pr_d, 1)
                        dve.tensor_tensor(sc_[:], raw[:, HC:2 * HC], raw[:, HC:2 * HC], ALU.mult).then_inc(pr_d, 1)
                        dve.wait_ge(pr_d, j.idx * 3 + 2)
                        dve.tensor_tensor(sa[:], sa[:], sc_[:], ALU.add).then_inc(pr_d, 1)
                    o, par, cpar, there = math_octet(j, s, conv, late)
                    tg = TG[par]
                    tfr, tfi, tf, ti = tg[:, :, 0:HC], tg[:, :, HC:C], tg[:, :, 0:C], tg[:, :, C:2 * C]
                    a = par_a[cpar]
                    ar = a[:, 0:HC].unsqueeze(1).broadcast_to([T, OS, HC])
                    a2 = a[:, 4 * HC:5 * HC].unsqueeze(1).broadcast_to([T, OS, HC])

                    def did(w):
                        w.then_inc(dv, 1)

                    def after(n, o=o):
                        dve.wait_ge(dv, o * NV + n)

                    if there:
                        dve.wait_ge(g_sb, o * OS + OS)
                        wait(dve, dv, o * NV)
                        wait(dve, am, o * NA)
                        did(dve.tensor_tensor(t0, tfr, tfi, ALU.add))
                        did(dve.scalar_tensor_tensor(d0, tfi, 1.0, a2, ALU.add, ALU.mult))
                        after(1)
                        did(dve.scalar_tensor_tensor(t0, t0, 2.0, ar, ALU.add, ALU.mult))
                        after(2)
                        did(dve.scalar_tensor_tensor(d0, tfr, 1.0, d0, ALU.add, ALU.mult))
                    if conv and s < NO:
                        oc = c.idx * NO + s
                        x2 = X2[s % NX]
                        dve.wait_ge(x2_ld[s % NX], (c.idx * len(range(s % NX, NO, NX)) + s // NX + 1) * 16)
                    for a_ in range(2):
                        if conv and s < NO:
                            dve.wait_ge(y_ps, oc * 2 + a_ + 1)
                            v = x2[:, Q * a_:Q * a_ + Q, :]
                            dve.scalar_tensor_tensor(v, pY[0:T, :].rearrange("t (b c) -> t b c", b=Q), 0.5, v,
                                                     ALU.mult, ALU.add).then_inc(x2_d, 1)
                        if there and a_ == 0:
                            dve.wait_ge(sp_d, o * 3 + 3)
                            did(dve.scalar_tensor_tensor(Dl[:], Z[:], 0.0, Dl[:], ALU.max, ALU.add))
                        if there and a_ == 1:
                            after(5)
                            did(dve.scalar_tensor_tensor(Dl[:], ti, 1.0, Dl[:], ALU.add, ALU.mult))
                    if conv and s < NO:
                        dve.wait_ge(x2_d, oc * 2 + 2)
                        wait(dve, ag_d, oc)
                        for i in range(OS):
                            w = dve.bn_stats(st[:, i, :], x2[:, i, :])
                        w.then_inc(st_d, 1)
                        dve.wait_ge(st_d, oc + 1)
                        wait(dve, rs_d, oc)
                        wait(dve, xn_d, oc)
                        moments(dve, st, mean[:], var[:], tmp[:], mo_d, oc * 2, ag_d)
                    if there:
                        after(6)
                        dve.wait_ge(bx_d, o + 1)
                        wait(dve, wv_d, o)
                        did(dve.tensor_tensor(IN[:], Dl[:], BX[:], ALU.mult))
                        dve.wait_ge(am, o * NA + 3)
                        did(dve.scalar_tensor_tensor(t1, d0, -2.0, t1, ALU.mult, ALU.add))
                    if conv and s < NO:
                        dve.wait_ge(rs_d, oc + 1)
                        wait(dve, bx_d, oc)
                        wait(dve, n_ps, oc * 2)
                        for i in range(OS):
                            w = dve.tensor_scalar(XN[:, i, :], x2[:, i, :], mean[:, i:i + 1], rst[:, i:i + 1],
                                                  ALU.subtract, ALU.mult)
                        w.then_inc(xn_d, 1)
                    if there:
                        dve.wait_ge(am, o * NA + 6)
                        did(dve.scalar_tensor_tensor(t2, d1, -2.0, t2, ALU.mult, ALU.add))
                    if there:
                        did(dve.scalar_tensor_tensor(q1, q1, -0.25, d1, ALU.add, ALU.subtract))
                        did(dve.scalar_tensor_tensor(d1, t1, 1.0, d1, ALU.add, ALU.mult))
                        after(9)
                        dve.wait_ge(am, o * NA + 7)
                        did(dve.scalar_tensor_tensor(c2, t2, 1.0, d2, ALU.add, ALU.mult))
                        did(dve.scalar_tensor_tensor(c1, q2, -0.25, d2, ALU.add, ALU.subtract))
                    if there:
                        after(13)
                        did(dve.scalar_tensor_tensor(q1, c1, 1.0, q1, ALU.add, ALU.mult))
                        after(13)
                        did(dve.scalar_tensor_tensor(d1, c1, 1.0, d1, ALU.add, ALU.mult))
                        after(14)
                        did(dve.scalar_tensor_tensor(q1, q1, 1.0, c2, ALU.add, ALU.subtract))
                        after(16)
                        did(dve.tensor_tensor(c2, c2, d1, ALU.add))
                        did(dve.scalar_tensor_tensor(q0, q0, -0.25, d0, ALU.add, ALU.subtract))
                        did(dve.scalar_tensor_tensor(d0, t0, 1.0, d0, ALU.add, ALU.mult))
                        after(18)
                        did(dve.tensor_tensor(q0, q1, q0, ALU.mult))
                        after(19)
                        did(dve.tensor_tensor(d0, q1, d0, ALU.mult))
                        after(20)
                        did(dve.scalar_tensor_tensor(q0, q0, 1.0, c2, ALU.add, ALU.subtract))
                        after(22)
                        did(dve.tensor_tensor(c2, c2, d0, ALU.add))
                        dve.wait_ge(wv_d, o + 1)
                        did(dve.scalar_tensor_tensor(Wv[:], tf, 1.0, Wv[:], ALU.add, ALU.mult))
                        after(24)

                        def both(v):
                            return v.unsqueeze(2).broadcast_to([T, OS, 2, HC])

                        def split(v):
                            return v.rearrange("t b (r c) -> t b r c", r=2)

                        did(dve.tensor_tensor(split(Wv[:]), split(Wv[:]), both(q0), ALU.mult))
                        dve.wait_ge(am, o * NA + 8)
                        did(dve.tensor_tensor(split(IN[:]), split(IN[:]), both(t1), ALU.mult))
                        after(26)
                        did(dve.tensor_tensor(Wv[:], Wv[:], IN[:], ALU.add))
                        after(27)
                        did(dve.scalar_tensor_tensor(Wv[:], X2[((s or NO) - 1) % NX][:], 0.5, Wv[:], ALU.add, ALU.add))
                    if scan and s == SLOTS - 2:
                        dve.wait_ge(th_d, j.idx + 1)
                        b0 = j.idx * 8
                        pa = par_a[j.par]
                        wait(dve, wp_d, (j.idx - 1) * NO)
                        dve.tensor_scalar(sa[:], sa[:], 1e-8, None, ALU.add).then_inc(pa_d, 1)
                        dve.wait_ge(pa_d, b0 + 1)
                        dve.reciprocal(sa[:], sa[:]).then_inc(pa_d, 1)
                        dve.wait_ge(pa_d, b0 + 2)
                        dve.scalar_tensor_tensor(sa[:], sc_[:], 1.0, sa[:], ALU.add, ALU.mult).then_inc(pa_d, 1)
                        dve.wait_ge(pa_d, b0 + 3)
                        k = 0.95 / 4
                        dve.scalar_tensor_tensor(pa[:, 0:HC], raw[:, 0:HC], k, sa[:], ALU.mult, ALU.mult)
                        dve.scalar_tensor_tensor(pa[:, HC:C], raw[:, 0:HC], k, sa[:], ALU.mult, ALU.mult)
                        dve.scalar_tensor_tensor(pa[:, C:3 * HC], raw[:, HC:C], -k, sa[:], ALU.mult, ALU.mult)
                        dve.scalar_tensor_tensor(pa[:, 3 * HC:4 * HC], raw[:, HC:C], k, sa[:], ALU.mult,
                                                 ALU.mult).then_inc(pa_d, 1)
                        dve.wait_ge(pa_d, b0 + 4)
                        dve.tensor_tensor(sa[:], pa[:, 0:HC], pa[:, 0:HC], ALU.mult).then_inc(pa_d, 1)
                        dve.tensor_tensor(sc_[:], pa[:, 3 * HC:4 * HC], pa[:, 3 * HC:4 * HC], ALU.mult).then_inc(pa_d, 1)
                        dve.wait_ge(pa_d, b0 + 6)
                        dve.tensor_tensor(pa[:, 4 * HC:5 * HC], sa[:], sc_[:], ALU.add).then_inc(pa_d, 2)
                        dve.wait_ge(pa_d, b0 + 8)

            chunks(body, dve)

        @block.scalar
        def _(act):
            act.wait_ge(ready, 2)
            act.wait_ge(dch, 14)
            act.wait_ge(pch, 1)
            t0, d0, t1, d1, t2, d2, q0, q1, q2, c1, c2 = (half[n][:] for n in (
                "t0", "d0", "t1", "d1", "t2", "d2", "q0", "q1", "q2", "q2", "t2"))

            def body(j, prep, scan, conv, late):
                n, c = j.step(1), j.step(-1)
                for s in range(SLOTS):
                    o, par, cpar, there = math_octet(j, s, conv, late)
                    oc = c.idx * NO + s
                    conv_s = conv and s < NO

                    def needs(k):
                        act.wait_ge(dv, o * NV + k)

                    for k in range(K):
                        if scan:
                            t = K * s + k
                            if t == 0:
                                wait(act, y_ps, c.idx * NO * 2)
                            act.wait_ge(z_ps, j.idx * T + t + 1)
                            act.activation(U[j.par][:, t, :], pW[t // R % 2][:, B * (t % R):B * (t % R) + B], ACT.Tanh,
                                           bias=zb[:, 0:1], scale=0.5).then_inc(u_sb, 1)
                        if prep and s < NO and k in (2, 4):
                            a = k // 2 - 1
                            act.wait_ge(xt_ps, (n.idx * NO + s) * 2 + a + 1)
                            wait(act, w_ps, j.idx * (T // R))
                            act.copy(XT[n.par][:, OS * s + Q * a:OS * s + Q * a + Q, :].rearrange("c b t -> c (b t)"),
                                     pX[:, 0:Q * T]).then_inc(xt_sb, 1)
                        if there and k == 1:
                            needs(3)
                            act.activation(t1, t0, ACT.Square).then_inc(am, 1)
                            act.activation(q0, t0, ACT.Square, bias=cols[0:T, 1:2]).then_inc(am, 1)
                        if there and k == 1:
                            needs(4)
                            act.activation(d1, d0, ACT.Square).then_inc(am, 1)
                        if there and k == 2:
                            act.wait_ge(am, o * NA + 3)
                            act.activation(d2, d1, ACT.Square).then_inc(am, 1)
                        if scan and s == SLOTS - 2 and k == 3:
                            act.wait_ge(mag_d, j.idx + 1)
                            act.activation(sc_[:], sa[:], ACT.Tanh, scale=0.5).then_inc(th_d, 1)
                        if there and k == 5:
                            needs(8)
                            act.activation(q1, t1, ACT.Square, bias=cols[0:T, 1:2]).then_inc(am, 1)
                            act.activation(t2, t1, ACT.Square).then_inc(am, 1)
                        if conv_s and k == 5:
                            for a, bank in enumerate((pN, pX)):
                                act.wait_ge(n_ps, oc * 2 + a + 1)
                                wait(act, g_ps, oc * OS)
                                act.copy(XNT[:, Q * a:Q * a + Q, :].rearrange("c b t -> c (b t)"),
                                         bank[:, 0:Q * T]).then_inc(n_sb, 1)
                        if there and k == 6:
                            needs(9)
                            act.activation(q2, t2, ACT.Square, bias=cols[0:T, 1:2]).then_inc(am, 1)
                        if there and k == K - 1:
                            needs(23)
                            act.activation(t1, c2, ACT.Identity, bias=cols[0:T, 0:1], scale=-1.0).then_inc(am, 1)
                        if conv_s and k > K - OS:
                            for i in range(k - (K - OS) - 1, OS if k == K - 1 else k - (K - OS)):
                                act.wait_ge(g_ps, oc * OS + i + 1)
                                if i == 0:
                                    wait(act, dv, (oc - 1) * NV)
                                    wait(act, dv, (oc - 1) * NV + 7)
                                act.activation(TG[s % 2][:, i, :], pG[i % 3][0:T, 0:2 * C], ACT.Tanh, scale=0.5)
                                act.copy(Z[:, i, :], pG[i % 3][0:T, 2 * C:3 * C]).then_inc(g_sb, 1)
                    if conv_s:
                        act.wait_ge(g_sb, oc * OS + OS)
                        act.activation(Dl[:], Z[:], ACT.Abs).then_inc(sp_d, 1)
                        act.wait_ge(sp_d, oc * 3 + 1)
                        act.activation(Dl[:], Dl[:], ACT.Exp, scale=-1.0).then_inc(sp_d, 1)
                        act.wait_ge(sp_d, oc * 3 + 2)
                        act.activation(Dl[:], Dl[:], ACT.Ln, bias=cols[0:T, 0:1]).then_inc(sp_d, 1)

            chunks(body, act)

        @block.tensor
        def _(pe):
            pe.wait_ge(cst, 16 * 16)
            pe.wait_ge(b3d, 48)
            pe.wait_ge(dch, 1)
            pe.matmul(pG[0][:, 0:C], gram[:, 0:C], wt, start=True, stop=True).then_inc(mmc, 1)
            pe.matmul(pG[1][:, 0:C], mb, wt, start=True, stop=True).then_inc(mmc, 1)
            pe.wait_ge(dch, 2)
            pe.matmul(pG[2][:, 0:C], onesm, ee, start=True, stop=True).then_inc(mmc, 1)
            pe.wait_ge(dch, 9)
            pe.matmul(pW[0][:, 0:C], onesm, vh[:], start=True, stop=True).then_inc(mmc, 1)
            pe.wait_ge(ready, 2)
            pe.wait_ge(pch, 1)
            pe.wait_ge(dch, 14)

            def inputs(j, r):
                if r == 0:
                    pe.wait_ge(xt_sb, (j.idx + 1) * NO * 2)
                wait(pe, u_sb, j.idx * T + R * (r - 1))
                pe.matmul(pW[r % 2][:, 0:R * B], ws[:], XT[j.par][:, :, R * r:R * r + R].rearrange("c b t -> c t b"),
                          start=True, stop=False, skip_group_check=True).then_inc(w_ps, 1)

            def turn_u(c, s, a):
                wait(pe, x2_d, (c.idx * NO + s) * 2 + a)
                for i in range(Q):
                    w = pe.transpose(pY[0:T, C * i:C * i + C], U[c.par][:, :, OS * s + Q * a + i], ident[:])
                w.then_inc(y_ps, 1)

            def body(j, prep, scan, conv, late):
                n, c = j.step(1), j.step(-1)
                if scan:
                    inputs(j, 0)
                for s in range(SLOTS):
                    oc = c.idx * NO + s
                    conv_s = conv and s < NO
                    for k in range(K):
                        if scan:
                            t = K * s + k
                            wait(pe, u_sb, j.idx * T + t)
                            before = U[j.par][:, t - 1, :] if t else U[1 - j.par][:, T - 1, :]
                            pe.matmul(pW[t // R % 2][:, B * (t % R):B * (t % R) + B], vh[:], before, start=False,
                                      stop=True, skip_group_check=True).then_inc(z_ps, 1)
                            if t % R == 2 and t // R + 1 < T // R:
                                inputs(j, t // R + 1)
                        if scan and s == SLOTS - 2 and k == 0:
                            pe.wait_ge(d_ld, j.idx * 16 + 16)
                            if conv_s:
                                pe.wait_ge(n_sb, oc * 2)
                            pe.matmul(pN[0:T, 0:4 * HC], D[:], kern[:], start=True, stop=True).then_inc(d_ps, 1)
                        if conv and s == 0 and k == 0:
                            pe.wait_ge(u_sb, j.idx * T)
                            turn_u(c, 0, 0)
                        if conv_s and k == 1:
                            turn_u(c, s, 1)
                        if conv and s + 1 < NO and k == K - 2:
                            turn_u(c, s + 1, 0)
                        if prep and s < NO and k in (1, 3):
                            a = k // 2
                            o = n.idx * NO + s
                            pe.wait_ge(xq_ld[a], o * 16 + 16)
                            wait(pe, xt_sb, o * 2 + a)
                            if conv:
                                wait(pe, n_sb, oc * 2)
                            for i in range(Q):
                                w = pe.transpose(pX[:, T * i:T * i + T], XQ[a][:, i, :], ident[0:T, 0:T])
                            w.then_inc(xt_ps, 1)
                        if conv_s and k == 5:
                            pe.wait_ge(xn_d, oc + 1)
                            if scan and s == SLOTS - 2:
                                pe.wait_ge(raw_d, j.idx + 1)
                            if prep:
                                pe.wait_ge(xt_sb, (n.idx * NO + s) * 2 + 2)
                            wait(pe, n_sb, oc * 2)
                            for a, bank in enumerate((pN, pX)):
                                for i in range(Q):
                                    w = pe.transpose(bank[:, T * i:T * i + T], XN[:, Q * a + i, :], ident[0:T, 0:T])
                                w.then_inc(n_ps, 1)
                        if conv_s and k >= K - OS:
                            for i in (k - (K - OS),):
                                if i % Q == 0:
                                    pe.wait_ge(n_sb, oc * 2 + i // Q + 1)
                                wait(pe, g_sb, oc * OS + max(i - 2, 0))
                                pe.matmul(pG[i % 3][0:T, 0:3 * C], XNT[:, i, :], wg[:], start=True, stop=False,
                                          skip_group_check=True)
                                pe.matmul(pG[i % 3][0:T, 0:3 * C], ones3[:], b3[:], start=False, stop=True,
                                          skip_group_check=True).then_inc(g_ps, 1)

            chunks(body, pe)


def expert_phase(nc, B, x3_d, gate_wT, gate_b, w1, b1, w2, ident_d, ones_d, wm_d, po_d, ox_d, out):
    NP = B // 2
    G = GT * T
    with ExitStack() as ctx:
        def sb(name, shape, dt=F32):
            return ctx.enter_context(nc.sbuf_tensor("e_" + name, shape, dt))

        def ps(name, shape):
            return ctx.enter_context(nc.psum_tensor("e_" + name, shape, F32))

        def sem(name):
            return ctx.enter_context(nc.semaphore("e_" + name))

        def pairs(body, eng):
            body(Image(0, 0, 0), True, False)
            if NP > 2:
                body(Image(1, 0, 1), True, True)
                if NP > 4:
                    with eng.Fori(0, (NP - 4) // 2) as i:
                        body(Image(i * 2 + 2, i + 1, 0), True, True)
                        body(Image(i * 2 + 3, i + 1, 1), True, True)
                body(Image(NP - 2, NP // 2 - 1, 0), True, True)
            body(Image(NP - 1, NP // 2 - 1, 1), True, True)
            body(Image(NP, NP // 2, 0), False, True)

        ident = sb("ident", [P, P])
        ones = sb("ones", [P, P])

        with ExitStack() as rt:
            def sb(name, shape, dt=F32):
                return rt.enter_context(nc.sbuf_tensor("r_" + name, shape, dt))

            def ps(name, shape):
                return rt.enter_context(nc.psum_tensor("r_" + name, shape, F32))

            def sem(name):
                return rt.enter_context(nc.semaphore("r_" + name))

            X = [[sb(f"X{p}{o}", [T, NT, C]) for o in range(2)] for p in range(2)]
            XT = [[sb(f"XT{a}{o}", [C, G]) for o in range(2)] for a in range(2)]
            Lg = [sb(f"Lg{p}", [P, S]) for p in range(2)]
            Ex = sb("Ex", [P, S])
            Lr = sb("Lr", [P, S])
            WT = sb("WT", [T, NT, P])
            PS = [sb(f"PS{o}", [C, E]) for o in range(2)]
            gw = sb("gw", [C, E])
            gb = sb("gb", [P, 1])
            m8 = sb("m8", [P, 8])
            nm = sb("nm", [P, 1])
            zs = sb("zs", [P, 1])
            st = sb("st", [T, NT, 6])
            mean = [sb(f"mean{o}", [T, NT]) for o in range(2)]
            var = [sb(f"var{o}", [T, NT]) for o in range(2)]
            tmp = sb("tmp", [T, NT])
            rst = [sb(f"rst{o}", [T, NT]) for o in range(2)]
            nhalf = sb("nhalf", [T, NT])
            epst = sb("epst", [T, NT])
            pT = [ps(f"pT{o}", [P, 512]) for o in range(2)]
            pL = [ps(f"pL{a}", [P, 512]) for a in range(2)]
            pM = [ps(f"pM{a}", [P, 512]) for a in range(2)]
            pP = [ps(f"pP{o}", [P, 512]) for o in range(2)]
            cst = sem("cst"); ini = sem("ini")
            x_ld = [[sem(f"x_ld{p}{o}") for o in range(2)] for p in range(2)]
            st_d = sem("st_d"); mo_d = sem("mo_d"); ag_d = sem("ag_d"); ep_d = sem("ep_d"); rs_d = sem("rs_d"); xn_d = sem("xn_d")
            xt_ps = sem("xt_ps"); xt_sb = sem("xt_sb"); l_ps = sem("l_ps"); l_sb = sem("l_sb")
            m_d = sem("m_d"); lr_d = sem("lr_d"); nm_d = sem("nm_d"); ex_d = sem("ex_d"); er_d = sem("er_d")
            df_d = sem("df_d"); rz_d = sem("rz_d"); wm_s = sem("wm_s"); wm_st = sem("wm_st")
            wt_ps = sem("wt_ps"); wt_sb = sem("wt_sb"); p_ps = sem("p_ps"); p_sb = sem("p_sb")
            po_st = [sem(f"po_st{o}") for o in range(2)]

            block = rt.enter_context(nc.Block())

            @block.sync
            def _(sp):
                sp.dma_start(ident[:], ident_d).then_inc(cst, 16)
                sp.dma_start(ones[:], ones_d).then_inc(cst, 16)
                sp.dma_start(gw[:], gate_wT).then_inc(cst, 16)
                for o in range(2):
                    sp.dma_start(gb[E * o:E * o + E, :], gate_b.rearrange("(e a) -> e a", a=1)).then_inc(cst, 16)

                def body(m, one, two):
                    if one:
                        for o in range(2):
                            wait(sp, p_ps, (m.idx - 1) * 2 - 1 + o)
                            sp.dma_start(X[m.par][o][:], x3_d[bass.ds(m.idx * 2 + o, 1), :, :]
                                         .rearrange("a (n t) c -> t (a n) c", t=T)).then_inc(x_ld[m.par][o], 16)
                    if two:
                        q = m.idx - 1
                        sp.wait_ge(wm_s, q + 1)
                        sp.dma_start(wm_d[bass.ds(q, 1), :, :].rearrange("a p s -> (a p) s"), Ex[:]).then_inc(wm_st, 16)
                        for o in range(2):
                            sp.wait_ge(p_sb, q * 2 + o + 1)
                            sp.dma_start(po_d[bass.ds(q * 2 + o, 1), :, :].rearrange("a c e -> (a c) e"),
                                         PS[o][:]).then_inc(po_st[o], 16)

                pairs(body, sp)
                sp.wait_ge(wm_st, NP * 16)
                for o in range(2):
                    sp.wait_ge(po_st[o], NP * 16)

            @block.gpsimd
            def _(pool):
                pool.memset(epst[:], 1e-5)
                pool.memset(nhalf[:], -0.5).then_inc(ini, 1)
                pool.wait_ge(ini, 1)

                def body(m, one, two):
                    if one:
                        for o in range(2):
                            b = m.idx * 2 + o
                            pool.wait_ge(ag_d, b + 1)
                            wait(pool, xn_d, (b - 1) * NG)
                            pool.tensor_tensor(rst[o][:], var[o][:], epst[:], ALU.add).then_inc(ep_d, 1)
                            pool.wait_ge(ep_d, b + 1)
                            pool.tensor_tensor(rst[o][:], rst[o][:], nhalf[:], ALU.pow).then_inc(rs_d, 1)
                    if two:
                        pool.wait_ge(er_d, m.idx)
                        pool.tensor_tensor(Ex[:], Ex[:], Lr[:], ALU.subtract).then_inc(df_d, 1)

                pairs(body, pool)

            @block.vector
            def _(dve):
                def body(m, one, two):
                    if two:
                        q = m.idx - 1
                        lg = Lg[1 - m.par]
                        dve.wait_ge(l_sb, q * NG + NG)
                        wait(dve, ex_d, q)
                    for o in range(2):
                        b = m.idx * 2 + o
                        if one:
                            dve.wait_ge(x_ld[m.par][o], m.half * 16 + 16)
                            wait(dve, ag_d, b)
                            for t in range(NT):
                                w = dve.bn_stats(st[:, t, :], X[m.par][o][:, t, :])
                            w.then_inc(st_d, 1)
                        if two and o == 0:
                            dve.max(m8[:], lg[:]).then_inc(m_d, 1)
                            wait(dve, df_d, q)
                            dve.wait_ge(m_d, q + 1)
                            dve.tensor_scalar(nm[:], m8[:, 0:1], -1.0, None, ALU.mult).then_inc(nm_d, 1)
                            dve.match_replace(Lr[:], m8[:], lg[:], -3e38).then_inc(lr_d, 1)
                        if one:
                            wait(dve, rs_d, b - 1)
                            wait(dve, xn_d, (b - 1) * NG)
                            dve.wait_ge(st_d, b + 1)
                            moments(dve, st, mean[o][:], var[o][:], tmp[:], mo_d, b * 2, ag_d)
                    if two:
                        dve.wait_ge(ex_d, q + 1)
                        dve.reciprocal(zs[:], zs[:]).then_inc(rz_d, 1)
                    if one:
                        for o in range(2):
                            b = m.idx * 2 + o
                            dve.wait_ge(rs_d, b + 1)
                            for t in range(NT):
                                v = X[m.par][o][:, t, :]
                                w = dve.tensor_scalar(v, v, mean[o][:, t:t + 1], rst[o][:, t:t + 1], ALU.subtract,
                                                      ALU.mult)
                                if t % GT == GT - 1:
                                    w.then_inc(xn_d, 1)
                    if two:
                        dve.wait_ge(df_d, q + 1)
                        dve.wait_ge(rz_d, q + 1)
                        dve.tensor_scalar(Ex[:], Ex[:], zs[:, 0:1], None, ALU.mult).then_inc(wm_s, 1)
                        wait(dve, p_ps, q * 2)
                        for k in range(NG):
                            dve.wait_ge(wt_ps, q * NG + k + 1)
                            dve.tensor_copy(WT[:, GT * k:GT * k + GT, :].rearrange("t n e -> t (n e)"),
                                            pM[k % 2][0:T, :]).then_inc(wt_sb, 1)
                        for o in range(2):
                            dve.wait_ge(p_ps, q * 2 + o + 1)
                            wait(dve, po_st[o], q * 16)
                            dve.tensor_copy(PS[o][:], pP[o][:, 0:E]).then_inc(p_sb, 1)

                pairs(body, dve)

            @block.scalar
            def _(act):
                act.wait_ge(cst, 80)

                def body(m, one, two):
                    if two:
                        q = m.idx - 1
                        lg = Lg[1 - m.par]
                        act.wait_ge(nm_d, q + 1)
                        wait(act, wm_st, q * 16)
                        wait(act, wt_ps, q * NG)
                        wait(act, wm_s, q)
                        act.activation(Ex[:], lg[:], ACT.Exp, bias=nm[:, 0:1], accum_out=zs[:, 0:1]).then_inc(ex_d, 1)
                        act.wait_ge(lr_d, q + 1)
                        act.activation(Lr[:], Lr[:], ACT.Exp, bias=nm[:, 0:1]).then_inc(er_d, 1)
                    if one:
                        for k in range(NG):
                            i = m.idx * NG + k
                            for o in range(2):
                                act.wait_ge(xt_ps, i * 2 + o + 1)
                                wait(act, l_ps, i - 1)
                                act.copy(XT[k % 2][o][:], pT[o][:, 0:G]).then_inc(xt_sb, 1)
                            act.wait_ge(l_ps, i + 1)
                            wait(act, lr_d, m.idx - 1)
                            act.activation(Lg[m.par][:, G * k:G * k + G], pL[k % 2][:, 0:G], ACT.Identity,
                                           bias=gb[:, 0:1]).then_inc(l_sb, 1)

                pairs(body, act)

            @block.tensor
            def _(pe):
                pe.wait_ge(cst, 80)

                def body(m, one, two):
                    if one:
                        for k in range(NG):
                            i = m.idx * NG + k
                            for o in range(2):
                                pe.wait_ge(xn_d, (m.idx * 2 + o) * NG + k + 1)
                                wait(pe, xt_sb, i * 2 + o - 1)
                                for t in range(GT):
                                    w = pe.transpose(pT[o][:, T * t:T * t + T], X[m.par][o][:, GT * k + t, :],
                                                     ident[0:T, 0:T])
                                w.then_inc(xt_ps, 1)
                            pe.wait_ge(xt_sb, i * 2 + 2)
                            wait(pe, l_sb, i - 1)
                            for o in range(2):
                                w = pe.matmul(pL[k % 2][E * o:E * o + E, 0:G], gw[:], XT[k % 2][o][:], start=True,
                                              stop=True)
                            w.then_inc(l_ps, 1)
                    if two:
                        q = m.idx - 1
                        pe.wait_ge(wm_s, q + 1)
                        for k in range(NG):
                            wait(pe, wt_sb, q * NG + k - 1)
                            for t in range(GT):
                                n = GT * k + t
                                w = pe.transpose(pM[k % 2][0:T, P * t:P * t + P], Ex[:, T * n:T * n + T], ident[:])
                            w.then_inc(wt_ps, 1)
                        pe.wait_ge(wt_sb, q * NG + NG)
                        for o in range(2):
                            wait(pe, p_sb, q * 2 - 1 + o)
                            for n in range(NT):
                                w = pe.matmul(pP[o][:, 0:E], X[1 - m.par][o][:, n, :], WT[:, n, E * o:E * o + E],
                                              start=n == 0, stop=n == NT - 1)
                            w.then_inc(p_ps, 1)

                pairs(body, pe)

        NH4 = HID // P
        with ExitStack() as ex:
            def sb(name, shape, dt=F32):
                return ex.enter_context(nc.sbuf_tensor("x_" + name, shape, dt))

            def ps(name, shape):
                return ex.enter_context(nc.psum_tensor("x_" + name, shape, F32))

            def sem(name):
                return ex.enter_context(nc.semaphore("x_" + name))

            PO = sb("PO", [C, B, E])
            W1 = [sb(f"W1{p}", [C, HID]) for p in range(2)]
            W2 = [sb(f"W2{p}", [P, NH4, C]) for p in range(2)]
            B2 = [sb(f"B2{p}", [1, C]) for p in range(2)]
            B1 = [sb(f"B1{p}", [P, NH4]) for p in range(2)]
            Hs = [sb(f"Hs{p}", [P, NH4, B]) for p in range(2)]
            OX = [sb(f"OX{p}", [B, C]) for p in range(2)]
            pH = [ps(f"pH{p}", [P, 512]) for p in range(2)]
            pZ = [ps(f"pZ{p}", [P, 512]) for p in range(2)]
            po_ld = sem("po_ld")
            w_ld = [sem(f"w_ld{p}") for p in range(2)]
            h_ps = sem("h_ps"); h_sb = sem("h_sb"); z_ps = sem("z_ps"); z_sb = sem("z_sb")
            ox_st = [sem(f"ox_st{p}") for p in range(2)]

            def experts(body, eng):
                body(Image(0, 0, 0), True, False)
                body(Image(1, 0, 1), True, True)
                body(Image(2, 1, 0), True, True)
                body(Image(3, 1, 1), True, True)
                with eng.Fori(0, (E - 4) // 2) as i:
                    body(Image(i * 2 + 4, i + 2, 0), True, True)
                    body(Image(i * 2 + 5, i + 2, 1), True, True)
                body(Image(E, E // 2, 0), False, True)

            block = ex.enter_context(nc.Block())

            @block.sync
            def _(sp):
                sp.dma_start(PO[:], po_d.rearrange("b c e -> c b e")).then_inc(po_ld, 16)

                def body(m, one, two):
                    if one:
                        wait(sp, z_ps, m.idx - 1)
                        e = bass.ds(m.idx, 1)
                        sp.dma_start(W1[m.par][:], w1[e, 0:C, :].rearrange("a d h -> (a d) h")).then_inc(w_ld[m.par], 16)
                        sp.dma_start(W2[m.par][:], w2[e, 0:HID, :].rearrange("a (k p) o -> p (a k) o", p=P)
                                     ).then_inc(w_ld[m.par], 16)
                        sp.dma_start(B1[m.par][:], b1[e, :, :].rearrange("a p k -> (a p) k")).then_inc(w_ld[m.par], 16)
                        sp.dma_start(B2[m.par][:], w2[e, HID:HID + 1, :].rearrange("a x o -> (a x) o")
                                     ).then_inc(w_ld[m.par], 16)

                experts(body, sp)
                for p in range(2):
                    sp.wait_ge(ox_st[p], E // 2 * 16)

            @block.tensor
            def _(pe):
                pe.wait_ge(po_ld, 16)

                def body(m, one, two):
                    if one:
                        pe.wait_ge(w_ld[m.par], m.half * 64 + 64)
                        wait(pe, h_sb, m.idx - 1)
                        for k in range(NH4):
                            w = pe.matmul(pH[m.par][:, B * k:B * k + B], W1[m.par][:, P * k:P * k + P],
                                          PO[:, :, bass.ds(m.idx, 1)].rearrange("c b a -> c (b a)"),
                                          start=True, stop=True)
                        w.then_inc(h_ps, 1)
                    if two:
                        p = 1 - m.par
                        pe.wait_ge(h_sb, m.idx)
                        wait(pe, z_sb, m.idx - 2)
                        for k in range(NH4):
                            pe.matmul(pZ[p][0:B, 0:C], Hs[p][:, k, :], W2[p][:, k, :], start=k == 0, stop=False)
                        pe.matmul(pZ[p][0:B, 0:C], ones[0:1, 0:B], B2[p][:], start=False, stop=True).then_inc(z_ps, 1)

                experts(body, pe)

            @block.scalar
            def _(act):
                def body(m, one, two):
                    if one:
                        act.wait_ge(h_ps, m.idx + 1)
                        wait(act, z_ps, m.idx - 1)
                        for k in range(NH4):
                            w = act.activation(Hs[m.par][:, k, :], pH[m.par][:, B * k:B * k + B], ACT.Gelu,
                                               bias=B1[m.par][:, k:k + 1])
                        w.then_inc(h_sb, 1)

                experts(body, act)

            @block.vector
            def _(dve):
                def body(m, one, two):
                    if two:
                        p = 1 - m.par
                        q = m.step(-1)
                        dve.wait_ge(z_ps, m.idx)
                        wait(dve, ox_st[p], q.half * 16)
                        dve.tensor_copy(OX[p][:], pZ[p][0:B, 0:C]).then_inc(z_sb, 1)

                experts(body, dve)

            @block.gpsimd
            def _(pool):
                def body(m, one, two):
                    if two:
                        p = 1 - m.par
                        pool.wait_ge(z_sb, m.idx)
                        pool.dma_start(ox_d[:, bass.ds(m.idx - 1, 1), :].rearrange("b a o -> b (a o)"),
                                       OX[p][:]).then_inc(ox_st[p], 16)

                experts(body, pool)

        with ExitStack() as sc:
            def sb(name, shape, dt=F32):
                return sc.enter_context(nc.sbuf_tensor("c_" + name, shape, dt))

            def ps(name, shape):
                return sc.enter_context(nc.psum_tensor("c_" + name, shape, F32))

            def sem(name):
                return sc.enter_context(nc.semaphore("c_" + name))

            X = [[sb(f"X{p}{o}", [T, NT, C]) for o in range(2)] for p in range(2)]
            Wm = [sb(f"Wm{p}", [P, S]) for p in range(2)]
            OX = [sb(f"OX{p}", [P, C]) for p in range(2)]
            pS = [ps(f"pS{a}", [P, 512]) for a in range(4)]
            x_ld = [[sem(f"x_ld{p}{o}") for o in range(2)] for p in range(2)]
            w_ld = [sem(f"w_ld{p}") for p in range(2)]
            s_ps = sem("s_ps"); s_sb = sem("s_sb")
            o_st = [sem(f"o_st{p}") for p in range(2)]

            def each(body, eng):
                body(Image(0, 0, 0))
                body(Image(1, 0, 1))
                if NP > 2:
                    with eng.Fori(0, (NP - 2) // 2) as i:
                        body(Image(i * 2 + 2, i + 1, 0))
                        body(Image(i * 2 + 3, i + 1, 1))

            block = sc.enter_context(nc.Block())

            @block.sync
            def _(sp):
                def body(m):
                    wait(sp, s_ps, (m.idx - 1) * 2 * NG)
                    sp.dma_start(Wm[m.par][:], wm_d[bass.ds(m.idx, 1), :, :].rearrange("a p s -> (a p) s")
                                 ).then_inc(w_ld[m.par], 16)
                    sp.dma_start(OX[m.par][:], ox_d[bass.ds(m.idx * 2, 2), :, :].rearrange("b e c -> (b e) c")
                                 ).then_inc(w_ld[m.par], 16)
                    wait(sp, o_st[m.par], m.half * 32)
                    for o in range(2):
                        sp.dma_start(X[m.par][o][:], x3_d[bass.ds(m.idx * 2 + o, 1), :, :]
                                     .rearrange("a (n t) c -> t (a n) c", t=T)).then_inc(x_ld[m.par][o], 16)

                each(body, sp)

            @block.scalar
            def _(act):
                def body(m):
                    for o in range(2):
                        act.wait_ge(s_sb, (m.idx * 2 + o) * NG + NG)
                        act.dma_start(out[bass.ds(m.idx * 2 + o, 1), :, :].rearrange("a (n t) c -> t (a n) c", t=T),
                                      X[m.par][o][:]).then_inc(o_st[m.par], 16)

                each(body, act)
                for p in range(2):
                    act.wait_ge(o_st[p], NP // 2 * 32)

            @block.tensor
            def _(pe):
                def body(m):
                    pe.wait_ge(w_ld[m.par], m.half * 32 + 32)
                    for o in range(2):
                        for k in range(NG):
                            i = (m.idx * 2 + o) * NG + k
                            bank = pS[(o * NG + k) % 2 + 2 * m.par]
                            wait(pe, s_sb, i - 1)
                            for t in range(GT):
                                n = GT * k + t
                                w = pe.matmul(bank[0:T, C * t:C * t + C], Wm[m.par][E * o:E * o + E, T * n:T * n + T],
                                              OX[m.par][E * o:E * o + E, :], start=True, stop=True)
                            w.then_inc(s_ps, 1)

                each(body, pe)

            @block.vector
            def _(dve):
                def body(m):
                    for o in range(2):
                        dve.wait_ge(x_ld[m.par][o], m.half * 16 + 16)
                        for k in range(NG):
                            i = (m.idx * 2 + o) * NG + k
                            bank = pS[(o * NG + k) % 2 + 2 * m.par]
                            v = X[m.par][o][:, GT * k:GT * k + GT, :].rearrange("t n c -> t (n c)")
                            dve.wait_ge(s_ps, i + 1)
                            dve.tensor_tensor(v, bank[0:T, :], v, ALU.add).then_inc(s_sb, 1)

                each(body, dve)


def metaformer(nc, B, A, x1_d, xh_d, x3_d, wm_d, po_d, ox_d, out):
    with ExitStack() as ctx:
        gram = ctx.enter_context(nc.sbuf_tensor("gram", [C, C + 1], F32))
        attention_phase(nc, B, A["x"], A["w_qkvT"], A["qkv_bias"], A["w_projT"], A["proj_bias"], A["rel_table"],
                        A["mask"], A["ident"], A["ones"], x1_d, xh_d, gram)
        scan_phase(nc, B, x1_d.rearrange("b h w c -> b (h w) c"), xh_d.rearrange("b h w c -> b (h w) c"), gram,
                   A["w_ffnT"], A["v_ffnT"], A["gamma"], A["beta"], A["w_gates"], A["b_gates"], A["dft"],
                   (A["A_re"], A["A_im"]), (A["B_re"], A["B_im"]), A["ident"], A["ones"], x3_d)
        expert_phase(nc, B, x3_d, A["gate_wT"], A["gate_b"], A["w1"], A["b1"], A["w2"], A["ident"], A["ones"],
                     wm_d, po_d, ox_d, out)


def window_mask():
    m = np.zeros((P, 4, L), np.float32)
    r, c = np.divmod(np.arange(L), WIN)
    for last in range(2):
        for column in range(2):
            for second in range(2):
                region = 2 * last * (r >= WIN - SHIFT) + (column and second) * (c >= WIN - SHIFT)
                m[64 * second:64 * second + L, 2 * last + column] = np.where(region[:, None] != region[None], -100.0, 0.0)
    return m


def dft_matrix(k):
    i, j = np.divmod(np.arange(k * k), k)
    u, v = np.divmod(np.arange(S), W)
    ph = (H - k) // 2
    turn = (u[None] * (ph + i[:, None]) + v[None] * (ph + j[:, None])) % W
    d = np.zeros((P, S), np.float32)
    d[:k * k] = np.cos(2 * np.pi * turn / W)
    d[64:64 + k * k] = np.sin(2 * np.pi * turn / W)
    return np.ascontiguousarray(d.reshape(P, NT, T).transpose(1, 0, 2))


def kernel(**inputs):
    import concourse.bacc as _bacc
    from concourse.bass_utils import run_bass_kernel_spmd as _run

    g = {k: np.asarray(v) for k, v in inputs.items()}

    def taps(name):
        return g[name].reshape(g[name].shape[0], -1).T

    b1 = g["L1_ffn_weight1"][:, C, :].reshape(E, HID // P, P).transpose(0, 2, 1)
    lay = {
        "x": g["x"],
        "w_qkvT": g["L0_conv_qkv_weight"].T, "qkv_bias": g["L0_conv_qkv_bias"],
        "w_projT": g["L0_conv_proj_weight"].T, "proj_bias": g["L0_conv_proj_bias"],
        "rel_table": g["L0_conv_rel_bias_table"][::-1].T,
        "w_ffnT": g["L0_ffn_W"].T, "v_ffnT": g["L0_ffn_V"].T,
        "gamma": g["L0_ffn_gamma"], "beta": g["L0_ffn_beta"],
        "w_gates": np.concatenate([g["L1_conv_Wf"], g["L1_conv_Wi"], g["L1_conv_Wd"]], 1),
        "b_gates": np.concatenate([g["L1_conv_bf"], g["L1_conv_bi"], g["L1_conv_bd"]]),
        "A_re": taps("L1_conv_A_real"), "A_im": taps("L1_conv_A_imag"),
        "B_re": taps("L1_conv_B_real"), "B_im": taps("L1_conv_B_imag"),
        "gate_wT": g["L1_ffn_gate_w"].T, "gate_b": g["L1_ffn_gate_b"],
        "w1": g["L1_ffn_weight1"], "b1": b1, "w2": g["L1_ffn_weight2"],
        "mask": window_mask(), "dft": dft_matrix(WIN),
        "ident": np.eye(P, dtype=np.float32), "ones": np.ones((P, P), np.float32),
    }
    B = g["x"].shape[0]
    nc = _bacc.Bacc("TRN2", target_bir_lowering=False, num_devices=1)
    arrays, aps = {}, {}
    for name, a in lay.items():
        arrays[f"in_{name}_dram"] = a = np.ascontiguousarray(a)
        aps[name] = nc.dram_tensor(f"in_{name}_dram", a.shape, mybir.dt.from_np(a.dtype), kind="ExternalInput").ap()

    def dram(name, shape, kind="Internal"):
        return nc.dram_tensor(name, shape, F32, kind=kind).ap()

    out = dram("out_dram", [B, S, C], "ExternalOutput")
    metaformer(nc, B, aps, dram("x1_dram", [B, H, W, C]), dram("xh_dram", [B, H, W, C]), dram("x3_dram", [B, S, C]),
               dram("wm_dram", [B // 2, P, S]), dram("po_dram", [B, C, E]), dram("ox_dram", [B, E, C]), out)
    r = _run(nc, [arrays], core_ids=[0])
    return r.results[0]["out_dram"].reshape(B, H, W, C)
```
